# Optimizing a Trainium2 kernel written in Bass

```python
import numpy as np
import jax
import jax.numpy as jnp

def _softmax(x, axis=-1):
    return jax.nn.softmax(x, axis=axis)

def _gelu(x):
    return jax.nn.gelu(x, approximate=True)

def _silu(x):
    return jax.nn.silu(x)

def _sigmoid(x):
    return jax.nn.sigmoid(x)

def _layernorm(x, axis=-1, eps=1e-05):
    m = jnp.mean(x, axis=axis, keepdims=True)
    v = jnp.var(x, axis=axis, keepdims=True)
    return (x - m) / jnp.sqrt(v + eps)

def _scatter_add(tgt, idx, src, axis=0):
    return tgt.at[idx].add(src)

def _segment_sum(src, seg, n):
    return jax.ops.segment_sum(src, seg, n)
kernel_name = 'mk_vit_tower_postln_d1_tok_img256_r4_776b69'

def setup_inputs(seed: int=0):
    np.random.seed(seed)
    _w = jnp.asarray

    def _rec_inputs():
        import jax
        import jax.numpy as jnp
        _rk = jax.random.key(seed)
        x = -0.00016672 + 0.999947 * jax.random.normal(jax.random.fold_in(_rk, 1), (16, 3, 96, 96), jnp.float32)
        return x
    x = _rec_inputs()

    def _L0_tok_setup():
        import jax, jax.numpy as jnp
        import numpy as np
        PATCH = 16
        key = jax.random.key(seed)
        k1, k2, k3 = jax.random.split(key, 3)
        B, C, H, Wd = (64, 3, 96, 96)
        E = 64
        pdim = PATCH * PATCH * C
        x = jax.random.normal(k1, (B, C, H, Wd), dtype=jnp.float32)
        W = jax.random.normal(k2, (E, pdim), dtype=jnp.float32) * pdim ** (-0.5)
        b = jax.random.normal(k3, (E,), dtype=jnp.float32) * 0.01
        return {'x': x, 'W': W, 'b': b}
    _L0_tok_all = _L0_tok_setup()
    _L0_tok_in = {k: v for k, v in _L0_tok_all.items() if k in ('W', 'b')}
    del _L0_tok_all

    def _L0_attn_setup():
        import jax, jax.numpy as jnp
        import numpy as np
        import math
        B, N, D = (4, 1024, 64)
        key = jax.random.key(seed)
        k0, k1, k2, k3 = jax.random.split(key, 4)
        bound = math.sqrt(6.0 / D)
        return {'x': jax.random.normal(k0, (B, N, D), dtype=jnp.float32), 'Wq': jax.random.uniform(k1, (D, D), dtype=jnp.float32, minval=-bound, maxval=bound), 'Wk': jax.random.uniform(k2, (D, D), dtype=jnp.float32, minval=-bound, maxval=bound), 'Wv': jax.random.uniform(k3, (D, D), dtype=jnp.float32, minval=-bound, maxval=bound)}
    _L0_attn_all = _L0_attn_setup()
    _L0_attn_in = {k: v for k, v in _L0_attn_all.items() if k in ('Wq', 'Wk', 'Wv')}
    del _L0_attn_all

    def _L0_ffn_setup():
        import jax, jax.numpy as jnp
        import numpy as np
        B, S, H, F, E, K = (8, 1024, 64, 128, 16, 2)
        EPS = 1e-05
        key = jax.random.key(seed)
        ks = jax.random.split(key, 9)
        sc = 0.02
        return {'x': jax.random.normal(ks[0], (B, S, H), dtype=jnp.float32), 'gate_w': jax.random.normal(ks[1], (H, E), dtype=jnp.float32) * sc, 'gate_b': jnp.zeros((E,), dtype=jnp.float32), 'w1': jax.random.normal(ks[2], (E, H, F), dtype=jnp.float32) * sc, 'b1': jnp.zeros((E, F), dtype=jnp.float32), 'w2': jax.random.normal(ks[3], (E, F, H), dtype=jnp.float32) * sc, 'b2': jnp.zeros((E, H), dtype=jnp.float32), 'gamma': jnp.ones((H,), dtype=jnp.float32), 'beta': jnp.zeros((H,), dtype=jnp.float32)}
    _L0_ffn_all = _L0_ffn_setup()
    _L0_ffn_in = {k: v for k, v in _L0_ffn_all.items() if k in ('gate_w', 'gate_b', 'w1', 'b1', 'w2', 'b2', 'gamma', 'beta')}
    del _L0_ffn_all
    return {'x': x, 'L0_tok_W': _L0_tok_in['W'], 'L0_tok_b': _L0_tok_in['b'], 'L0_attn_Wq': _L0_attn_in['Wq'], 'L0_attn_Wk': _L0_attn_in['Wk'], 'L0_attn_Wv': _L0_attn_in['Wv'], 'L0_ffn_gate_w': _L0_ffn_in['gate_w'], 'L0_ffn_gate_b': _L0_ffn_in['gate_b'], 'L0_ffn_w1': _L0_ffn_in['w1'], 'L0_ffn_b1': _L0_ffn_in['b1'], 'L0_ffn_w2': _L0_ffn_in['w2'], 'L0_ffn_b2': _L0_ffn_in['b2'], 'L0_ffn_gamma': _L0_ffn_in['gamma'], 'L0_ffn_beta': _L0_ffn_in['beta']}

def reference(x, L0_tok_W, L0_tok_b, L0_attn_Wq, L0_attn_Wk, L0_attn_Wv, L0_ffn_gate_w, L0_ffn_gate_b, L0_ffn_w1, L0_ffn_b1, L0_ffn_w2, L0_ffn_b2, L0_ffn_gamma, L0_ffn_beta):
    import jax
    import jax.numpy as jnp

    def _L0_tok_ref(x, W, b):
        import jax, jax.numpy as jnp
        import numpy as np
        PATCH = 16
        B, C, H, Wd = x.shape
        p = PATCH
        nH, nW = (H // p, Wd // p)
        patches = x.reshape(B, C, nH, p, nW, p)
        patches = patches.transpose(0, 2, 4, 1, 3, 5)
        patches = patches.reshape(B, nH * nW, C * p * p)
        return jnp.einsum('bnk,ek->bne', patches, W) + b

    def _L0_attn_ref(x, Wq, Wk, Wv):
        import jax, jax.numpy as jnp
        import numpy as np
        import math
        B, N, D = (4, 1024, 64)
        q = x @ Wq.T
        k = x @ Wk.T
        v = x @ Wv.T
        n = x.shape[1]
        d_k = x.shape[2]
        mask = jnp.triu(jnp.ones((n, n), dtype=x.dtype), k=1)
        scale = jnp.asarray(1.0 / math.sqrt(d_k), dtype=x.dtype)
        s = (jnp.einsum('bnd,bmd->bnm', q, k) - (1.0 - mask) * 10000000000.0) * scale
        s = jax.nn.softmax(s, axis=1)
        return jnp.einsum('bnm,bmd->bnd', s, v)

    def _L0_ffn_ref(x, gate_w, gate_b, w1, b1, w2, b2, gamma, beta):
        import jax, jax.numpy as jnp
        import numpy as np
        B, S, H, F, E, K = (8, 1024, 64, 128, 16, 2)
        EPS = 1e-05
        gate_logits = x @ gate_w + gate_b
        topk_vals, topk_idx = jax.lax.top_k(gate_logits, K)
        topk_w = jax.nn.softmax(topk_vals, axis=-1)
        h = jax.nn.relu(jnp.einsum('bsh,ehf->bsef', x, w1) + b1)
        expert_out = jnp.einsum('bsef,efh->bseh', h, w2) + b2
        sel = jnp.take_along_axis(expert_out, topk_idx[:, :, :, None], axis=2)
        moe = jnp.sum(topk_w[..., None] * sel, axis=2)
        y = x + moe
        mu = jnp.mean(y, axis=-1, keepdims=True)
        var = jnp.var(y, axis=-1, keepdims=True)
        return (y - mu) / jnp.sqrt(var + EPS) * gamma + beta
    h = _L0_tok_ref(x, L0_tok_W, L0_tok_b)
    h = _layernorm(h + _L0_attn_ref(h, L0_attn_Wq, L0_attn_Wk, L0_attn_Wv), axis=-1)
    h = _layernorm(h + _L0_ffn_ref(h, L0_ffn_gate_w, L0_ffn_gate_b, L0_ffn_w1, L0_ffn_b1, L0_ffn_w2, L0_ffn_b2, L0_ffn_gamma, L0_ffn_beta), axis=-1)
    return h

_drawn_inputs = setup_inputs


def setup_inputs(seed=0):
    import zlib

    import numpy as np

    out = dict(_drawn_inputs(seed))
    spreads = {'L0_ffn_gate_b': (0.0, 0.1),
     'L0_ffn_b1': (0.0, 0.8),
     'L0_ffn_b2': (0.0, 0.284),
     'L0_ffn_gamma': (1.0, 0.2),
     'L0_ffn_beta': (0.0, 0.1)}
    factors = {'L0_tok_b': 3.612, 'L0_ffn_w1': 7.205, 'L0_ffn_w2': 5.336}
    for name, (base, spread) in spreads.items():
        noise = np.random.default_rng([zlib.crc32(name.encode()), seed]).standard_normal(out[name].shape)
        drawn = base * np.exp(spread * noise) if base else spread * noise
        out[name] = jnp.asarray(drawn.astype(out[name].dtype))
    for name, factor in factors.items():
        out[name] = (out[name] * factor).astype(out[name].dtype)
    return out
```

```python
from contextlib import ExitStack

import concourse.bass as bass
from concourse import mybir

F32 = mybir.dt.float32
F32R = mybir.dt.float32r
U32 = mybir.dt.uint32
ALU = mybir.AluOpType
ACT = mybir.ActivationFunctionType
AX_X = mybir.AxisListType.X

PATCH = 16
TOPK = 2
EPS = 1e-5
MASKED = -1.0e10
OTHER_IMAGE = -1.0e30


def vit_tower(nc: bass.Bass, x_kt, tokw, qk, wvgb, w1, w2b1, b2, rows, out):
    P, HALVES, CH, HT = x_kt.shape
    D = tokw.shape[2] // 2
    E, F = w1.shape[1], w1.shape[2]
    N = out.shape[1]
    TT = 2 * N
    NT = HT // TT
    PAIRS = E // 2
    SCALE = float(D) ** -0.5
    assert P == 2 * D == F and NT * TT == HT and out.shape[0] * N == HALVES * HT

    with ExitStack() as ctx:
        def sb(name, shape, dt=F32):
            return ctx.enter_context(nc.sbuf_tensor(name, shape, dt))

        def sem(name):
            return ctx.enter_context(nc.semaphore(name))

        xk = sb("xk", [P, HALVES, CH, HT])
        tokw_sb = sb("tokw_sb", [P, CH, 2 * D])
        qk_sb = sb("qk_sb", [D, 3 * D])
        wvgb_sb = sb("wvgb_sb", [P, D + E + 1])
        w1_sb = sb("w1_sb", [P, E, F])
        w2b1_sb = sb("w2b1_sb", [F, E * D + E])
        b2_sb = sb("b2_sb", [E, D])
        rows_sb = sb("rows_sb", [TT, E + 2 * D])
        w2_sb = w2b1_sb[:, 0:E * D].rearrange("f (e d) -> f e d", e=E)
        tok_b = wvgb_sb[:, D + E:D + E + 1]
        gate_b, gamma, beta = rows_sb[:, 0:E], rows_sb[:, E:E + D], rows_sb[:, E + D:E + 2 * D]

        ident = sb("ident", [P, P])
        ident2 = sb("ident2", [P, D])
        ident2_r = sb("ident2_r", [P, D], F32R)
        mask = sb("mask", [TT, TT])
        iota_e = sb("iota_e", [TT, E])

        a_hi = sb("a_hi", [P, 2, D], F32R)
        a_lo = sb("a_lo", [P, 2, D], F32R)
        wvg = sb("wvg", [P, 2, D + E], F32R)
        w1_hi = sb("w1_hi", [P, E, F], F32R)
        w1_lo = sb("w1_lo", [P, E, F], F32R)

        hT = sb("hT", [P, HALVES, HT], F32R)
        tT = sb("tT", [P, HALVES, HT])
        s_sb = sb("s_sb", [TT, HALVES, NT, TT])
        e_sb = sb("e_sb", [TT, HALVES, NT, TT])
        smax = sb("smax", [TT, HALVES, NT])
        ssum = sb("ssum", [TT, HALVES, NT])
        srec = sb("srec", [TT, HALVES, NT])
        vs = sb("vs", [TT, HALVES, NT, D])
        y1 = sb("y1", [TT, HALVES, NT, D])
        y1s = sb("y1s", [TT, HALVES, NT, 2, D], F32R)
        y1T = sb("y1T", [P, HALVES, HT], F32R)
        lg = sb("lg", [TT, HALVES, NT, E])
        top = sb("top", [TT, HALVES, NT, 8])
        topi = sb("topi", [TT, HALVES, NT, 8], U32)
        topf = sb("topf", [TT, HALVES, NT, 8])
        gd = sb("gd", [TT, HALVES, 4, NT])
        one1 = sb("one1", [TT, HALVES, NT, E])
        one2 = sb("one2", [TT, HALVES, NT, E])
        g = sb("g", [TT, HALVES, NT, E])
        gT = sb("gT", [E, HALVES, HT])
        grow = sb("grow", [1, HALVES, E * HT])
        gb = sb("gb", [P, HALVES, E, HT])
        NH = 3
        hid = sb("hid", [F, NH, 2, HT])
        moe = sb("moe", [P, HALVES, HT])
        ybeta = sb("ybeta", [TT, HALVES, NT, D])
        stats = sb("stats", [TT, HALVES, 3, NT, 6])
        mv = sb("mv", [TT, HALVES, 3, NT, 2])
        rstd = sb("rstd", [TT, HALVES, 3, NT])
        rvar = sb("rvar", [TT, HALVES, 3, NT])
        power = sb("power", [TT, NT])
        cen = sb("cen", [TT, HALVES, 3, NT, D])
        y2 = sb("y2", [TT, HALVES, NT, D])
        n2 = sb("n2", [TT, HALVES, NT, D])
        n2g = sb("n2g", [TT, HALVES, NT, D])
        y3 = sb("y3", [TT, HALVES, NT, D])
        fin = sb("fin", [TT, HALVES, NT, D])

        banks = ctx.enter_context(nc.psum_tensor("banks", [P, 8, 512], F32))

        def tok_tiles(bank, width):
            return banks[0:TT, bank, 0:NT * width].rearrange("p (t d) -> p t d", t=NT)

        p_a = banks[:, 4, 0:D]
        p_h = [banks[:, b, 0:HT] for b in (0, 5)]
        p_t = [banks[:, b, 0:HT] for b in (1, 6)]
        p_s = [tok_tiles(b, TT) for b in (2, 7)]
        p_v = [tok_tiles(b, D) for b in (3, 5)]
        p_y = [tok_tiles(b, D) for b in (0, 6)]
        p_yT = [banks[:, b, 0:HT] for b in (1, 7)]
        p_lg = [tok_tiles(b, 2 * E) for b in (2, 5)]
        p_gT = [banks[0:E, b, 0:HT] for b in (3, 6)]
        p_moe = [banks[:, b, 0:HT] for b in (4, 5)]
        p_fin = [tok_tiles(b, D) for b in (7, 6)]
        p_hid = banks[:, 0:4, 0:HT]

        x_in = [[sem(f"x_in{h}{c}") for c in range(3)] for h in range(HALVES)]
        tokw_in, qk_in, wvgb_in, w1_in, w2_in, b2_in, rows_in = (
            sem(n) for n in ("tokw_in", "qk_in", "wvgb_in", "w1_in", "w2_in", "b2_in", "rows_in"))
        pool_step, consts = sem("pool_step"), sem("consts")
        ident2_r_ready = sem("ident2_r_ready")
        a_psum, a_hi_ready, a_lo_ready = sem("a_psum"), sem("a_hi_ready"), sem("a_lo_ready")
        wvg_hi_ready, wvg_lo_ready = sem("wvg_hi_ready"), sem("wvg_lo_ready")
        w1_hi_ready, w1_lo_ready = sem("w1_hi_ready"), sem("w1_lo_ready")
        h_psum, h_hi, h_lo = sem("h_psum"), sem("h_hi"), sem("h_lo")
        t_psum, t_ready = sem("t_psum"), sem("t_ready")
        s_psum, s_less_max, e_ready = sem("s_psum"), sem("s_less_max"), sem("e_ready")
        v_psum, vs_ready, y_psum = sem("v_psum"), sem("vs_ready"), sem("y_psum")
        y1_ready, y1_hi, y1_lo = sem("y1_ready"), sem("y1_hi"), sem("y1_lo")
        yT_psum, yT_ready = sem("yT_psum"), sem("yT_ready")
        lg_psum, lg_ready, gd_ready, ge_ready = sem("lg_psum"), sem("lg_ready"), sem("gd_ready"), sem("ge_ready")
        g_ready, gT_psum, gT_ready = sem("g_ready"), sem("gT_psum"), sem("gT_ready")
        grow_in = [sem(f"grow_in{h}") for h in range(HALVES)]
        gb_ready = sem("gb_ready")
        hid_psum, hid_relu, hid_ready, hid_used = sem("hid_psum"), sem("hid_relu"), sem("hid_ready"), sem("hid_used")
        moe_psum, moe_ready, fin_psum, fin_ready = sem("moe_psum"), sem("moe_ready"), sem("fin_psum"), sem("fin_ready")
        dve_step = sem("dve_step")
        var_ready, rstd_ready = sem("var_ready"), sem("rstd_ready")
        out_done = sem("out_done")

        GB = 4
        out_v = out.rearrange("b n d -> (b n) d").rearrange("(h t p) d -> h p t d", h=HALVES, t=NT)

        def bc(ap, shape):
            return ap.to_broadcast(shape)

        block = ctx.enter_context(nc.Block())

        @block.sync
        def _(sp):
            step = CH // 3
            sp.dma_start(tokw_sb[:, :, :], tokw).then_inc(tokw_in, 16)
            for h in range(HALVES):
                for c in range(3):
                    sp.dma_start(xk[:, h, step * c:step * (c + 1), :],
                                 x_kt[:, h, step * c:step * (c + 1), :]).then_inc(x_in[h][c], 16)
            sp.dma_start(w2b1_sb[:, :], w2b1).then_inc(w2_in, 16)
            for h in range(HALVES):
                sp.wait_ge(gT_ready, h + 1)
                sp.dma_start(grow[0:1, h, :].rearrange("o (e n) -> o e n", e=E),
                             gT[:, h, :]).then_inc(grow_in[h], 16)
            for h in range(HALVES):
                sp.wait_ge(fin_ready, h + 1)
                sp.dma_start(out_v[h], fin[:, h, :, :]).then_inc(out_done, 16)
            sp.wait_ge(out_done, 16 * HALVES)

        @block.gpsimd
        def _(pool):
            nc.gpsimd.memset(ident[:, :], 0.0).then_inc(pool_step, 1)
            nc.gpsimd.memset(ident2[:, :], 0.0).then_inc(pool_step, 1)
            nc.gpsimd.memset(mask[:, :], 0.0).then_inc(pool_step, 1)
            nc.gpsimd.memset(power[:, :], -0.5).then_inc(pool_step, 1)
            nc.gpsimd.iota(iota_e[:, :], pattern=[[1, E]], base=0, channel_multiplier=0,
                           allow_small_or_imprecise_dtypes=True).then_inc(consts, 1)
            pool.wait_ge(pool_step, 4)
            nc.gpsimd.affine_select(out=ident[:, :], in_=ident[:, :], compare_op=ALU.not_equal, fill=1.0,
                                    base=0, pattern=[[-1, P]], channel_multiplier=1).then_inc(consts, 1)
            nc.gpsimd.affine_select(out=ident2[:, :], in_=ident2[:, :], compare_op=ALU.not_equal, fill=1.0,
                                    base=0, pattern=[[-1, D]], channel_multiplier=1).then_inc(pool_step, 1)
            nc.gpsimd.affine_select(out=mask[:, :], in_=mask[:, :], compare_op=ALU.is_gt, fill=MASKED,
                                    base=0, pattern=[[-1, TT]], channel_multiplier=1).then_inc(pool_step, 1)
            pool.wait_ge(pool_step, 6)
            nc.gpsimd.affine_select(out=ident2[:, :], in_=ident2[:, :], compare_op=ALU.not_equal, fill=1.0,
                                    base=-D, pattern=[[-1, D]], channel_multiplier=1).then_inc(consts, 1)
            nc.gpsimd.affine_select(out=mask[:, 0:N], in_=mask[:, 0:N], compare_op=ALU.is_ge, fill=OTHER_IMAGE,
                                    base=N - 1, pattern=[[0, N]], channel_multiplier=-1).then_inc(consts, 1)
            nc.gpsimd.affine_select(out=mask[:, N:TT], in_=mask[:, N:TT], compare_op=ALU.is_ge, fill=OTHER_IMAGE,
                                    base=-N, pattern=[[0, N]], channel_multiplier=1).then_inc(consts, 1)
            pool.wait_ge(w1_hi_ready, 2)
            nc.gpsimd.tensor_tensor(w1_lo[:, :, :], w1_sb[:, :, :], w1_hi[:, :, :].bitcast(F32),
                                    ALU.subtract).then_inc(w1_lo_ready, 1)
            norms = [0]

            def inverse_deviation(h, k):
                norms[0] += 1
                pool.wait_ge(var_ready, norms[0])
                nc.gpsimd.tensor_tensor(rstd[:, h, k, :], rvar[:, h, k, :], power[:, :],
                                        ALU.pow).then_inc(rstd_ready, 1)

            inverse_deviation(0, 0)
            inverse_deviation(1, 0)
            for h in range(HALVES):
                pool.wait_ge(grow_in[h], 16)
                for q in range(E // GB):
                    nc.gpsimd.partition_broadcast(
                        gb[:, h, GB * q:GB * (q + 1), :].rearrange("p e n -> p (e n)"),
                        grow[0:1, h, GB * HT * q:GB * HT * (q + 1)], P).then_inc(gb_ready, 1)
            for h in range(HALVES):
                inverse_deviation(h, 1)
                inverse_deviation(h, 2)

        @block.scalar
        def _(act):
            act.dma_start(qk_sb[:, :], qk).then_inc(qk_in, 16)
            for r in range(2):
                act.dma_start(wvgb_sb[D * r:D * (r + 1), :], wvgb).then_inc(wvgb_in, 16)
            act.dma_start(rows_sb[:, :], rows.partition_broadcast(TT)).then_inc(rows_in, 16)
            act.dma_start(b2_sb[:, :], b2).then_inc(b2_in, 16)
            for r in range(2):
                act.dma_start(w1_sb[D * r:D * (r + 1), :, :], w1).then_inc(w1_in, 16)
            act.wait_ge(consts, 5)
            nc.scalar.copy(ident2_r[:, :], ident2[:, :]).then_inc(ident2_r_ready, 1)
            act.wait_ge(wvgb_in, 32)
            nc.scalar.copy(wvg[:, 0, :], wvgb_sb[:, 0:D + E]).then_inc(wvg_hi_ready, 1)
            act.wait_ge(a_psum, 1)
            nc.scalar.copy(a_hi[:, :, :], bc(p_a.unsqueeze(1), [P, 2, D])).then_inc(a_hi_ready, 1)

            def tokens_hi(h):
                act.wait_ge(h_psum, h + 1)
                nc.scalar.activation(hT[:, h, :], p_h[h], ACT.Identity, bias=tok_b).then_inc(h_hi, 1)

            def t_copy(h):
                act.wait_ge(t_psum, h + 1)
                nc.scalar.copy(tT[:, h, :], p_t[h]).then_inc(t_ready, 1)

            def exps(h):
                act.wait_ge(s_less_max, h + 1)
                nc.scalar.activation(e_sb[:, h, :, :], s_sb[:, h, :, :], ACT.Exp, scale=SCALE).then_inc(e_ready, 1)

            def y1_split(h):
                act.wait_ge(y1_ready, h + 1)
                nc.scalar.copy(y1s[:, h, :, 0, :], y1[:, h, :, :]).then_inc(y1_hi, 1)

            def yT_copy(h):
                act.wait_ge(yT_psum, h + 1)
                nc.scalar.copy(y1T[:, h, :], p_yT[h]).then_inc(yT_ready, 1)

            def gate_exp(h):
                act.wait_ge(gd_ready, h + 1)
                nc.scalar.activation(gd[:, h, 1, :], gd[:, h, 0, :], ACT.Exp).then_inc(ge_ready, 1)

            def gT_copy(h):
                act.wait_ge(gT_psum, h + 1)
                nc.scalar.copy(gT[:, h, :], p_gT[h]).then_inc(gT_ready, 1)

            def relu(h, p):
                for e in (2 * p, 2 * p + 1):
                    act.wait_ge(hid_psum, h * E + e + 1)
                    nc.scalar.activation(p_hid[:, e % 4, :], p_hid[:, e % 4, :], ACT.Relu,
                                         bias=w2b1_sb[:, E * D + e:E * D + e + 1]).then_inc(hid_relu, 1)

            def moe_copy(h):
                act.wait_ge(moe_psum, h + 1)
                nc.scalar.copy(moe[:, h, :], p_moe[h]).then_inc(moe_ready, 1)

            tokens_hi(0)
            t_copy(0)
            act.wait_ge(w1_in, 32)
            nc.scalar.copy(w1_hi[:, 0:E // 2, :], w1_sb[:, 0:E // 2, :]).then_inc(w1_hi_ready, 1)
            exps(0)
            tokens_hi(1)
            t_copy(1)
            nc.scalar.copy(w1_hi[:, E // 2:E, :], w1_sb[:, E // 2:E, :]).then_inc(w1_hi_ready, 1)
            y1_split(0)
            yT_copy(0)
            exps(1)
            gate_exp(0)
            act.wait_ge(w2_in, 16)
            gT_copy(0)
            relu(0, 0)
            y1_split(1)
            relu(0, 1)
            yT_copy(1)
            relu(0, 2)
            gate_exp(1)
            relu(0, 3)
            gT_copy(1)
            for p in range(4, PAIRS):
                relu(0, p)
            moe_copy(0)
            for p in range(PAIRS):
                relu(1, p)
            moe_copy(1)

        @block.vector
        def _(dve):
            steps = [0]
            norms = [0]

            def step(ins):
                steps[0] += 1
                ins.then_inc(dve_step, 1)
                return steps[0]

            def tokens_lo(h):
                dve.wait_ge(h_hi, h + 1)
                lo = hT[D:P, h, :]
                nc.vector.scalar_tensor_tensor(out=lo, in0=p_h[h][D:P, :], scalar=tok_b[D:P, :],
                                               in1=lo.bitcast(F32), op0=ALU.add,
                                               op1=ALU.subtract).then_inc(h_lo, 1)

            def softmax_in(h):
                shape = [TT, NT, TT]
                dve.wait_ge(s_psum, h + 1)
                n = step(nc.vector.tensor_tensor(s_sb[:, h, :, :], p_s[h], bc(mask[:, :].unsqueeze(1), shape), ALU.add))
                dve.wait_ge(dve_step, n)
                n = step(nc.vector.tensor_reduce(smax[:, h, :], s_sb[:, h, :, :], AX_X, ALU.max))
                dve.wait_ge(dve_step, n)
                nc.vector.tensor_tensor(s_sb[:, h, :, :], s_sb[:, h, :, :], bc(smax[:, h, :].unsqueeze(2), shape),
                                        ALU.subtract).then_inc(s_less_max, 1)

            def values(h):
                dve.wait_ge(e_ready, h + 1)
                n = step(nc.vector.tensor_reduce(ssum[:, h, :], e_sb[:, h, :, :], AX_X, ALU.add))
                dve.wait_ge(dve_step, n)
                n = step(nc.vector.reciprocal(srec[:, h, :], ssum[:, h, :]))
                dve.wait_ge(dve_step, n)
                dve.wait_ge(v_psum, h + 1)
                nc.vector.tensor_tensor(vs[:, h, :, :], p_v[h], bc(srec[:, h, :].unsqueeze(2), [TT, NT, D]),
                                        ALU.mult).then_inc(vs_ready, 1)

            def layernorm(h, k, src, dst):
                for t in range(NT):
                    n = step(nc.vector.bn_stats(stats[:, h, k, t, :], src[:, t, :]))
                dve.wait_ge(dve_step, n)
                for t in range(NT):
                    n = step(nc.vector.bn_aggr(mv[:, h, k, t, :], stats[:, h, k, t, :]))
                dve.wait_ge(dve_step, n)
                nc.vector.tensor_scalar(rvar[:, h, k, :], mv[:, h, k, :, 1], EPS, None, ALU.add).then_inc(var_ready, 1)
                n = step(nc.vector.tensor_tensor(cen[:, h, k, :, :], src, bc(mv[:, h, k, :, 0:1], [TT, NT, D]),
                                                 ALU.subtract))
                dve.wait_ge(dve_step, n)
                norms[0] += 1
                dve.wait_ge(rstd_ready, norms[0])
                return nc.vector.tensor_tensor(dst, cen[:, h, k, :, :],
                                               bc(rstd[:, h, k, :].unsqueeze(2), [TT, NT, D]), ALU.mult)

            def norm1(h):
                dve.wait_ge(y_psum, h + 1)
                layernorm(h, 0, p_y[h], y1[:, h, :, :]).then_inc(y1_ready, 1)
                dve.wait_ge(y1_ready, h + 1)
                dve.wait_ge(y1_hi, h + 1)
                nc.vector.tensor_tensor(y1s[:, h, :, 1, :], y1[:, h, :, :], y1s[:, h, :, 0, :].bitcast(F32),
                                        ALU.subtract).then_inc(y1_lo, 1)

            def gates(h):
                dve.wait_ge(lg_psum, h + 1)
                n = step(nc.vector.tensor_tensor(one1[:, h, :, :], p_lg[h][:, :, 0:E],
                                                 bc(gate_b.unsqueeze(1), [TT, NT, E]), ALU.add))
                dve.wait_ge(dve_step, n)
                nc.vector.tensor_tensor(lg[:, h, :, :], p_lg[h][:, :, E:2 * E], one1[:, h, :, :],
                                        ALU.add).then_inc(lg_ready, 1)
                dve.wait_ge(lg_ready, h + 1)
                for t in range(NT):
                    n = step(nc.vector.max(top[:, h, t, :], lg[:, h, t, :]))
                dve.wait_ge(dve_step, n)
                nc.vector.tensor_tensor(gd[:, h, 0, :], top[:, h, :, 1], top[:, h, :, 0],
                                        ALU.subtract).then_inc(gd_ready, 1)
                for t in range(NT):
                    n = step(nc.vector.max_index(topi[:, h, t, :], top[:, h, t, :], lg[:, h, t, :]))
                dve.wait_ge(dve_step, n)
                n = step(nc.vector.tensor_copy(topf[:, h, :, :], topi[:, h, :, :]))
                dve.wait_ge(dve_step, n)
                shape = [TT, NT, E]
                numbers = bc(iota_e[:, :].unsqueeze(1), shape)
                step(nc.vector.tensor_tensor(one1[:, h, :, :], numbers, bc(topf[:, h, :, 0:1], shape), ALU.is_equal))
                step(nc.vector.tensor_tensor(one2[:, h, :, :], numbers, bc(topf[:, h, :, 1:2], shape), ALU.is_equal))
                dve.wait_ge(ge_ready, h + 1)
                n = step(nc.vector.tensor_scalar(gd[:, h, 3, :], gd[:, h, 1, :], 1.0, None, ALU.add))
                dve.wait_ge(dve_step, n)
                n = step(nc.vector.reciprocal(gd[:, h, 2, :], gd[:, h, 3, :]))
                dve.wait_ge(dve_step, n)
                n = step(nc.vector.tensor_tensor(gd[:, h, 3, :], gd[:, h, 1, :], gd[:, h, 2, :], ALU.mult))
                step(nc.vector.tensor_tensor(one1[:, h, :, :], one1[:, h, :, :],
                                             bc(gd[:, h, 2, :].unsqueeze(2), shape), ALU.mult))
                dve.wait_ge(dve_step, n)
                n = step(nc.vector.tensor_tensor(one2[:, h, :, :], one2[:, h, :, :],
                                                 bc(gd[:, h, 3, :].unsqueeze(2), shape), ALU.mult))
                dve.wait_ge(dve_step, n)
                nc.vector.tensor_tensor(g[:, h, :, :], one1[:, h, :, :], one2[:, h, :, :],
                                        ALU.add).then_inc(g_ready, 1)

            def gate_hidden(h, p):
                i = h * PAIRS + p
                dve.wait_ge(hid_relu, 2 * i + 2)
                dve.wait_ge(gb_ready, h * (E // GB) + 2 * p // GB + 1)
                if i >= NH:
                    dve.wait_ge(hid_used, i - NH + 1)
                b = 2 * (p % 2)
                nc.vector.tensor_tensor(hid[:, i % NH, :, :], p_hid[:, b:b + 2, :], gb[:, h, 2 * p:2 * p + 2, :],
                                        ALU.mult).then_inc(hid_ready, 1)

            def tail(h):
                dve.wait_ge(fin_psum, h + 1)
                n = step(nc.vector.tensor_tensor(y2[:, h, :, :], p_fin[h], y1[:, h, :, :], ALU.add))
                dve.wait_ge(dve_step, n)
                n = step(layernorm(h, 1, y2[:, h, :, :], n2[:, h, :, :]))
                dve.wait_ge(dve_step, n)
                shape = [TT, NT, D]
                n = step(nc.vector.tensor_tensor(n2g[:, h, :, :], n2[:, h, :, :], bc(gamma.unsqueeze(1), shape),
                                                 ALU.mult))
                dve.wait_ge(dve_step, n)
                n = step(nc.vector.tensor_tensor(y3[:, h, :, :], n2g[:, h, :, :], ybeta[:, h, :, :], ALU.add))
                dve.wait_ge(dve_step, n)
                layernorm(h, 2, y3[:, h, :, :], fin[:, h, :, :]).then_inc(fin_ready, 1)

            def y1_beta(h):
                step(nc.vector.tensor_tensor(ybeta[:, h, :, :], y1[:, h, :, :],
                                             bc(beta.unsqueeze(1), [TT, NT, D]), ALU.add))

            dve.wait_ge(wvg_hi_ready, 1)
            nc.vector.tensor_tensor(wvg[:, 1, :], wvgb_sb[:, 0:D + E], wvg[:, 0, :].bitcast(F32),
                                    ALU.subtract).then_inc(wvg_lo_ready, 1)
            dve.wait_ge(a_hi_ready, 1)
            nc.vector.tensor_tensor(a_lo[:, :, :], bc(p_a.unsqueeze(1), [P, 2, D]), a_hi[:, :, :].bitcast(F32),
                                    ALU.subtract).then_inc(a_lo_ready, 1)
            dve.wait_ge(consts, 5)
            dve.wait_ge(rows_in, 16)
            tokens_lo(0)
            softmax_in(0)
            tokens_lo(1)
            values(0)
            softmax_in(1)
            norm1(0)
            values(1)
            gates(0)
            norm1(1)
            y1_beta(0)
            gate_hidden(0, 0)
            gate_hidden(0, 1)
            gates(1)
            gate_hidden(0, 2)
            y1_beta(1)
            for p in range(3, PAIRS):
                gate_hidden(0, p)
            gate_hidden(1, 0)
            gate_hidden(1, 1)
            tail(0)
            for p in range(2, PAIRS):
                gate_hidden(1, p)
            tail(1)

        @block.tensor
        def _(pe):
            def embed(h):
                for c in range(CH):
                    if c % 2 == 0:
                        pe.wait_ge(x_in[h][c // 2], 16)
                    mm = nc.tensor.matmul(p_h[h], tokw_sb[:, c, :], xk[:, h, c, :],
                                          start=(c == 0), stop=(c == CH - 1))
                mm.then_inc(h_psum, 1)

            def project(h):
                pe.wait_ge(h_lo, h + 1)
                nc.tensor.matmul(p_t[h], a_hi[:, :, :].rearrange("p a d -> p (a d)"), hT[:, h, :], start=True, stop=False)
                nc.tensor.matmul(p_t[h], a_lo[:, :, :].rearrange("p a d -> p (a d)"), hT[:, h, :], start=False, stop=True).then_inc(t_psum, 1)

            def scores(h):
                pe.wait_ge(t_ready, h + 1)
                for t in range(NT):
                    cols = slice(TT * t, TT * (t + 1))
                    mm = nc.tensor.matmul(p_s[h][:, t, :], hT[:, h, cols].bitcast(F32), tT[:, h, cols],
                                          start=True, stop=True)
                mm.then_inc(s_psum, 1)

            def value_rows(h):
                for t in range(NT):
                    keys = hT[:, h, TT * t:TT * (t + 1)]
                    nc.tensor.matmul(p_v[h][:, t, :], keys, wvg[:, 0, 0:D], start=True, stop=False)
                    mm = nc.tensor.matmul(p_v[h][:, t, :], keys, wvg[:, 1, 0:D], start=False, stop=True)
                mm.then_inc(v_psum, 1)

            def attend(h):
                pe.wait_ge(vs_ready, h + 1)
                for t in range(NT):
                    nc.tensor.matmul(p_y[h][:, t, :], hT[:, h, TT * t:TT * (t + 1)], ident2_r[:, :],
                                     start=True, stop=False)
                    mm = nc.tensor.matmul(p_y[h][:, t, :], e_sb[:, h, t, :], vs[:, h, t, :], start=False, stop=True)
                mm.then_inc(y_psum, 1)

            def y1_transpose(h):
                pe.wait_ge(y1_lo, h + 1)
                for t in range(NT):
                    mm = nc.tensor.transpose(p_yT[h][:, TT * t:TT * (t + 1)],
                                             y1s[:, h, t, :, :].rearrange("p a d -> p (a d)").bitcast(F32),
                                             ident[0:TT, 0:TT])
                mm.then_inc(yT_psum, 1)

            def logits(h):
                pe.wait_ge(yT_ready, h + 1)
                for t in range(NT):
                    mm = nc.tensor.matmul(p_lg[h][:, t, :].rearrange("p (a e) -> p a e", a=2),
                                          y1T[:, h, TT * t:TT * (t + 1)], wvg[:, :, D:D + E], start=True, stop=True)
                mm.then_inc(lg_psum, 1)

            def gates_transpose(h):
                pe.wait_ge(g_ready, h + 1)
                for t in range(NT):
                    mm = nc.tensor.transpose(p_gT[h][:, TT * t:TT * (t + 1)], g[:, h, t, :], ident[0:TT, 0:TT])
                mm.then_inc(gT_psum, 1)

            def expert_in(h, p):
                i = h * PAIRS + p
                if i >= 2:
                    pe.wait_ge(hid_ready, i - 1)
                for e in (2 * p, 2 * p + 1):
                    nc.tensor.matmul(p_hid[:, e % 4, :], w1_hi[:, e, :], y1T[:, h, :], start=True, stop=False)
                    nc.tensor.matmul(p_hid[:, e % 4, :], w1_lo[:, e, :], y1T[:, h, :],
                                     start=False, stop=True).then_inc(hid_psum, 1)

            def expert_out(h, p):
                i = h * PAIRS + p
                pe.wait_ge(hid_ready, i + 1)
                for j in range(2):
                    mm = nc.tensor.matmul(p_moe[h][D * j:D * (j + 1), :], w2_sb[:, 2 * p + j, :],
                                          hid[:, i % NH, j, :], start=(p == 0), stop=(p == PAIRS - 1))
                mm.then_inc(hid_used, 1)
                if p == PAIRS - 1:
                    pe.wait_ge(hid_used, i + 1)
                    pe.sem_inc(moe_psum, 1)

            def combine(h):
                pe.wait_ge(moe_ready, h + 1)
                for t in range(NT):
                    cols = slice(TT * t, TT * (t + 1))
                    nc.tensor.matmul(p_fin[h][:, t, :], gT[:, h, cols], b2_sb[:, :], start=True, stop=False)
                    mm = nc.tensor.matmul(p_fin[h][:, t, :], moe[:, h, cols], ident2[:, :], start=False, stop=True)
                mm.then_inc(fin_psum, 1)

            pe.wait_ge(qk_in, 16)
            nc.tensor.matmul(p_a, qk_sb[:, 0:2 * D], qk_sb[:, 2 * D:3 * D], start=True, stop=True).then_inc(a_psum, 1)
            pe.wait_ge(tokw_in, 16)
            embed(0)
            pe.wait_ge(a_hi_ready, 1)
            pe.wait_ge(a_lo_ready, 1)
            project(0)
            scores(0)
            pe.wait_ge(wvg_lo_ready, 1)
            value_rows(0)
            embed(1)
            project(1)
            pe.wait_ge(ident2_r_ready, 1)
            attend(0)
            scores(1)
            value_rows(1)
            pe.wait_ge(consts, 5)
            y1_transpose(0)
            logits(0)
            attend(1)
            pe.wait_ge(w1_lo_ready, 1)
            expert_in(0, 0)
            gates_transpose(0)
            pe.wait_ge(gT_ready, 1)
            expert_in(0, 1)
            pe.wait_ge(w2_in, 16)
            pe.wait_ge(b2_in, 16)
            y1_transpose(1)
            logits(1)
            expert_out(0, 0)
            expert_in(0, 2)
            expert_out(0, 1)
            expert_in(0, 3)
            gates_transpose(1)
            for p in range(2, PAIRS):
                expert_out(0, p)
                if p + 2 < PAIRS:
                    expert_in(0, p + 2)
                else:
                    expert_in(1, p + 2 - PAIRS)
            pe.wait_ge(gT_ready, 2)
            for p in range(PAIRS):
                expert_out(1, p)
                if p + 2 < PAIRS:
                    expert_in(1, p + 2)
                if p == 0:
                    combine(0)
            combine(1)


def kernel(**inputs):
    import numpy as np
    import concourse.bacc as bacc
    from concourse.bass_utils import run_bass_kernel_spmd

    a = {k: np.asarray(v) for k, v in inputs.items()}
    x = a["x"]
    B, C, H, W = x.shape
    nh, nw = H // PATCH, W // PATCH
    D, K = a["L0_tok_W"].shape
    E, _, F = a["L0_ffn_w1"].shape
    tokens = B * nh * nw
    ch = K // 128
    xt = x.reshape(B, C, nh, PATCH, nw, PATCH).transpose(1, 3, 5, 0, 2, 4).reshape(ch, 128, 2, tokens // 2)
    arrays = {
        "x_kt": xt.transpose(1, 2, 0, 3),
        "tokw": np.concatenate([a["L0_tok_W"].T.reshape(ch, 128, D)] * 2, axis=2).transpose(1, 0, 2),
        "qk": np.concatenate([a["L0_attn_Wq"], a["L0_attn_Wq"], a["L0_attn_Wk"]], axis=1),
        "wvgb": np.concatenate([a["L0_attn_Wv"].T, a["L0_ffn_gate_w"], a["L0_tok_b"][:, None]], axis=1),
        "w1": a["L0_ffn_w1"].transpose(1, 0, 2),
        "w2b1": np.concatenate([a["L0_ffn_w2"].transpose(1, 0, 2).reshape(F, E * D), a["L0_ffn_b1"].T], axis=1),
        "b2": a["L0_ffn_b2"],
        "rows": np.concatenate([a["L0_ffn_gate_b"], a["L0_ffn_gamma"], a["L0_ffn_beta"]]),
    }
    arrays = {k: np.ascontiguousarray(v) for k, v in arrays.items()}
    nc = bacc.Bacc("TRN2", target_bir_lowering=False, num_devices=1)
    args = [nc.dram_tensor(k, v.shape, mybir.dt.from_np(v.dtype), kind="ExternalInput").ap()
            for k, v in arrays.items()]
    out = nc.dram_tensor("out", (B, nh * nw, D), F32, kind="ExternalOutput").ap()
    vit_tower(nc, *args, out)
    r = run_bass_kernel_spmd(nc, [arrays], core_ids=[0])
    return r.results[0]["out"]
```

```python
from contextlib import ExitStack

import concourse.bass as bass
from concourse import mybir

F32 = mybir.dt.float32
F32R = mybir.dt.float32r
U32 = mybir.dt.uint32
ALU = mybir.AluOpType
ACT = mybir.ActivationFunctionType
AX_X = mybir.AxisListType.X

PATCH = 16
TOPK = 2
WARM = 9
K0, K1, K2, K3, K4 = 9, 4, 2, 2, 8
EPS = 1e-5
MASKED = -1.0e10
OTHER_IMAGE = -1.0e30


def vit_tower(nc: bass.Bass, x_kt, tokw, qk, wvgb, w1, w2b1, b2, rows, out):
    P, HALVES, CH, HT = x_kt.shape
    D = tokw.shape[2]
    E, F = w1.shape[1], w1.shape[2]
    N = out.shape[1]
    TT = 2 * N
    NT = HT // TT
    PAIRS = E // 2
    SCALE = float(D) ** -0.5
    assert P == 2 * D == F and NT * TT == HT and out.shape[0] * N == HALVES * HT

    with ExitStack() as ctx:
        def sb(name, shape, dt=F32):
            return ctx.enter_context(nc.sbuf_tensor(name, shape, dt))

        def sem(name):
            return ctx.enter_context(nc.semaphore(name))

        xk = sb("xk", [P, HALVES, CH, HT])
        tokw_sb = sb("tokw_sb", [P, CH, 2, D])
        qk_sb = sb("qk_sb", [D, 3 * D])
        wvgb_sb = sb("wvgb_sb", [P, D + E + 1])
        w1_sb = sb("w1_sb", [P, E, F])
        w2b1_sb = sb("w2b1_sb", [F, E * D + E])
        b2_sb = sb("b2_sb", [E, D])
        rows_sb = sb("rows_sb", [TT, E + 2 * D])
        w2_sb = w2b1_sb[:, 0:E * D].rearrange("f (e d) -> f e d", e=E)
        tok_b = wvgb_sb[:, D + E:D + E + 1]
        gate_b, gamma, beta = rows_sb[:, 0:E], rows_sb[:, E:E + D], rows_sb[:, E + D:E + 2 * D]

        ident = sb("ident", [P, P])
        ident2 = sb("ident2", [P, D])
        ident2_r = sb("ident2_r", [P, D], F32R)
        mask = sb("mask", [TT, TT])
        iota_e = sb("iota_e", [TT, E])

        a_hi = sb("a_hi", [P, 2, D], F32R)
        a_lo = sb("a_lo", [P, 2, D], F32R)
        wvg = sb("wvg", [P, 2, D + E], F32R)
        w1_hi = sb("w1_hi", [P, E, F], F32R)
        w1_lo = sb("w1_lo", [P, E, F], F32R)

        hT = sb("hT", [P, HALVES, HT], F32R)
        tT = sb("tT", [P, HALVES, HT])
        s_sb = sb("s_sb", [TT, HALVES, NT, TT])
        e_sb = sb("e_sb", [TT, HALVES, NT, TT])
        smax = sb("smax", [TT, HALVES, NT])
        ssum = sb("ssum", [TT, HALVES, NT])
        srec = sb("srec", [TT, HALVES, NT])
        vs = sb("vs", [TT, HALVES, NT, D])
        y1 = sb("y1", [TT, HALVES, NT, D])
        y1s = sb("y1s", [TT, HALVES, NT, 2, D], F32R)
        y1T = sb("y1T", [P, HALVES, HT], F32R)
        lg = sb("lg", [TT, HALVES, NT, E])
        top = sb("top", [TT, HALVES, NT, 8])
        topi = sb("topi", [TT, HALVES, NT, 8], U32)
        lgb = sb("lgb", [TT, HALVES, NT, E])
        tope = sb("tope", [TT, HALVES, NT, TOPK])
        gsum = sb("gsum", [TT, HALVES, NT])
        grec = sb("grec", [TT, HALVES, NT])
        hot = sb("hot", [TT, HALVES, NT, TOPK, E])
        gun = sb("gun", [TT, HALVES, NT, E])
        g = sb("g", [TT, HALVES, NT, E])
        gT = sb("gT", [E, HALVES, HT])
        grow = sb("grow", [1, HALVES, E * HT])
        gb = sb("gb", [P, HALVES, E, HT])
        NH = 6
        hid = sb("hid", [F, NH, HT])
        moe = sb("moe", [P, HALVES, HT])
        ybeta = sb("ybeta", [TT, HALVES, NT, D])
        stats = sb("stats", [TT, HALVES, 3, NT, 6])
        mv = sb("mv", [TT, HALVES, 3, NT, 2])
        rstd = sb("rstd", [TT, HALVES, 3, NT])
        dev = sb("dev", [TT, HALVES, 3, NT])
        eps_t = sb("eps_t", [TT, 1])
        zeros = sb("zeros", [P, 512], mybir.dt.bfloat16)
        loaded = sb("loaded", [1, 8])
        bwarm = sb("bwarm", [P, 8])
        eps_row = sb("eps_row", [1, 8])
        cen = sb("cen", [TT, HALVES, 3, NT, D])
        n2g = sb("n2g", [TT, HALVES, NT, D])
        y3 = sb("y3", [TT, HALVES, NT, D])
        fin = sb("fin", [TT, HALVES, NT, D])

        banks = ctx.enter_context(nc.psum_tensor("banks", [P, 8, 512], F32))

        def tok_tiles(bank, width):
            return banks[0:TT, bank, 0:NT * width].rearrange("p (t d) -> p t d", t=NT)

        p_a = banks[:, 4, 0:D]
        p_h = [banks[:, b, 0:HT] for b in (0, 5)]
        p_t = [banks[:, b, 0:HT] for b in (1, 6)]
        p_s = [tok_tiles(b, TT) for b in (2, 7)]
        p_v = [tok_tiles(b, D) for b in (3, 5)]
        p_y = [tok_tiles(b, D) for b in (0, 6)]
        p_yT = [banks[:, b, 0:HT] for b in (1, 7)]
        p_lg = [tok_tiles(b, 2 * E) for b in (2, 5)]
        p_gT = [banks[0:E, b, 0:HT] for b in (3, 6)]
        p_moe = [banks[:, b, 0:HT] for b in (4, 5)]
        p_fin = [tok_tiles(b, D) for b in (7, 6)]
        p_hid = banks[:, 0:4, 0:HT]

        x_in = [[sem(f"x_in{h}{c}") for c in range(3)] for h in range(HALVES)]
        tokw_in, qk_in, wvgb_in, w1_in, w2_in, b2_in, rows_in = (
            sem(n) for n in ("tokw_in", "qk_in", "wvgb_in", "w1_in", "w2_in", "b2_in", "rows_in"))
        pool_step, consts = sem("pool_step"), sem("consts")
        ident2_r_ready = sem("ident2_r_ready")
        a_psum, a_hi_ready, a_lo_ready = sem("a_psum"), sem("a_hi_ready"), sem("a_lo_ready")
        wvg_hi_ready, wvg_lo_ready = sem("wvg_hi_ready"), sem("wvg_lo_ready")
        w1_hi_ready, w1_lo_ready = sem("w1_hi_ready"), sem("w1_lo_ready")
        h_psum, h_hi, h_lo = sem("h_psum"), sem("h_hi"), sem("h_lo")
        t_psum, t_ready = sem("t_psum"), sem("t_ready")
        s_psum, s_less_max, e_ready = sem("s_psum"), sem("s_less_max"), sem("e_ready")
        v_psum, vs_ready, y_psum = sem("v_psum"), sem("vs_ready"), sem("y_psum")
        y1_lo = sem("y1_lo")
        yT_psum, yT_ready = sem("yT_psum"), sem("yT_ready")
        lg_psum, lg_ready, gd_ready, ge_ready = sem("lg_psum"), sem("lg_ready"), sem("gd_ready"), sem("ge_ready")
        hot_ready = sem("hot_ready")
        g_ready, gT_psum, gT_ready = sem("g_ready"), sem("gT_psum"), sem("gT_ready")
        grow_in = [sem(f"grow_in{h}") for h in range(HALVES)]
        gb_ready = sem("gb_ready")
        hid_psum, hid_relu, hid_ready, hid_used = sem("hid_psum"), sem("hid_relu"), sem("hid_ready"), sem("hid_used")
        moe_ready, fin_psum, fin_ready = sem("moe_ready"), sem("fin_psum"), sem("fin_ready")
        dve_step = sem("dve_step")
        ybeta_ready = sem("ybeta_ready")
        mv_ready, dev_ready = sem("mv_ready"), sem("dev_ready")
        zeros_ready, tokw_doubled = sem("zeros_ready"), sem("tokw_doubled")
        out_done = sem("out_done")

        BCASTS = (0, 2, 4, 8, 12, E)
        out_v = out.rearrange("b n d -> (b n) d").rearrange("(h t p) d -> h p t d", h=HALVES, t=NT)

        def bc(ap, shape):
            return ap.to_broadcast(shape)

        def mv_count(h, k):
            return h + 1 if k == 0 else HALVES + 2 * h + k

        block = ctx.enter_context(nc.Block())

        @block.sync
        def _(sp):
            step = CH // 3
            sp.dma_start(tokw_sb[:, :, 0, :], tokw).then_inc(tokw_in, 16)
            for h in range(HALVES):
                for c in range(3):
                    sp.dma_start(xk[:, h, step * c:step * (c + 1), :],
                                 x_kt[:, h, step * c:step * (c + 1), :]).then_inc(x_in[h][c], 16)
            for r in range(2):
                sp.dma_start(w1_sb[D * r:D * (r + 1), :, :], w1).then_inc(w1_in, 16)
            sp.dma_start(rows_sb[:, :], rows.partition_broadcast(TT)).then_inc(rows_in, 16)
            sp.dma_start(w2b1_sb[:, :], w2b1).then_inc(w2_in, 16)
            sp.dma_start(b2_sb[:, :], b2).then_inc(b2_in, 16)
            for h in range(HALVES):
                sp.wait_ge(gT_ready, h + 1)
                sp.dma_start(grow[0:1, h, :].rearrange("o (e n) -> o e n", e=E),
                             gT[:, h, :]).then_inc(grow_in[h], 16)
            for h in range(HALVES):
                sp.wait_ge(fin_ready, h + 1)
                sp.dma_start(out_v[h], fin[:, h, :, :]).then_inc(out_done, 16)
            sp.wait_ge(out_done, 16 * HALVES)

        @block.gpsimd
        def _(pool):
            nc.gpsimd.memset(ident[:, :], 0.0).then_inc(pool_step, 1)
            nc.gpsimd.memset(ident2[:, :], 0.0).then_inc(pool_step, 1)
            nc.gpsimd.memset(mask[:, :], 0.0).then_inc(pool_step, 1)
            nc.gpsimd.memset(eps_row[:, :], EPS).then_inc(pool_step, 1)
            nc.gpsimd.memset(eps_t[:, :], EPS).then_inc(pool_step, 1)
            nc.gpsimd.iota(iota_e[:, :], pattern=[[1, E]], base=0, channel_multiplier=0,
                           allow_small_or_imprecise_dtypes=True).then_inc(consts, 1)
            pool.wait_ge(pool_step, 5)
            nc.gpsimd.affine_select(out=ident[:, :], in_=ident[:, :], compare_op=ALU.not_equal, fill=1.0,
                                    base=0, pattern=[[-1, P]], channel_multiplier=1).then_inc(consts, 1)
            nc.gpsimd.affine_select(out=ident2[:, :], in_=ident2[:, :], compare_op=ALU.not_equal, fill=1.0,
                                    base=0, pattern=[[-1, D]], channel_multiplier=1).then_inc(pool_step, 1)
            nc.gpsimd.affine_select(out=mask[:, :], in_=mask[:, :], compare_op=ALU.is_gt, fill=MASKED,
                                    base=0, pattern=[[-1, TT]], channel_multiplier=1).then_inc(pool_step, 1)
            pool.wait_ge(pool_step, 7)
            nc.gpsimd.affine_select(out=ident2[:, :], in_=ident2[:, :], compare_op=ALU.not_equal, fill=1.0,
                                    base=-D, pattern=[[-1, D]], channel_multiplier=1).then_inc(consts, 1)
            nc.gpsimd.affine_select(out=mask[:, 0:N], in_=mask[:, 0:N], compare_op=ALU.is_ge, fill=OTHER_IMAGE,
                                    base=N - 1, pattern=[[0, N]], channel_multiplier=-1).then_inc(consts, 1)
            nc.gpsimd.affine_select(out=mask[:, N:TT], in_=mask[:, N:TT], compare_op=ALU.is_ge, fill=OTHER_IMAGE,
                                    base=-N, pattern=[[0, N]], channel_multiplier=1).then_inc(consts, 1)
            nc.gpsimd.partition_broadcast(bwarm[:, :], eps_row[0:1, :], P).then_inc(pool_step, 1)
            for k in range(2):
                es = slice(E // 2 * k, E // 2 * (k + 1))
                pool.wait_ge(w1_hi_ready, k + 1)
                nc.gpsimd.tensor_tensor(w1_lo[:, es, :], w1_sb[:, es, :], w1_hi[:, es, :].bitcast(F32),
                                        ALU.subtract).then_inc(w1_lo_ready, 1)
            for h in range(HALVES):
                pool.wait_ge(grow_in[h], 16)
                for e0, e1 in zip(BCASTS, BCASTS[1:]):
                    nc.gpsimd.partition_broadcast(
                        gb[:, h, e0:e1, :].rearrange("p e n -> p (e n)"),
                        grow[0:1, h, HT * e0:HT * e1], P).then_inc(gb_ready, e1 - e0)
                if h == 0:
                    pool.wait_ge(rows_in, 16)
                pool.wait_ge(y1_lo, h + 1)
                nc.gpsimd.tensor_tensor(ybeta[:, h, :, :], y1[:, h, :, :], bc(beta.unsqueeze(1), [TT, NT, D]),
                                        ALU.add).then_inc(ybeta_ready, 1)

        @block.scalar
        def _(act):
            act.dma_start(qk_sb[:, :], qk).then_inc(qk_in, 16)
            for r in range(2):
                act.dma_start(wvgb_sb[D * r:D * (r + 1), :], wvgb).then_inc(wvgb_in, 16)
            act.wait_ge(consts, 5)
            nc.scalar.copy(ident2_r[:, :], ident2[:, :]).then_inc(ident2_r_ready, 1)
            act.wait_ge(wvgb_in, 32)
            nc.scalar.copy(wvg[:, 0, :], wvgb_sb[:, 0:D + E]).then_inc(wvg_hi_ready, 1)
            act.wait_ge(a_psum, 1)
            nc.scalar.copy(a_hi[:, :, :], bc(p_a.unsqueeze(1), [P, 2, D])).then_inc(a_hi_ready, 1)

            def tokens_hi(h):
                act.wait_ge(h_psum, h + 1)
                nc.scalar.activation(hT[:, h, :], p_h[h], ACT.Identity, bias=tok_b).then_inc(h_hi, 1)

            def t_copy(h):
                act.wait_ge(t_psum, h + 1)
                nc.scalar.copy(tT[:, h, :], p_t[h]).then_inc(t_ready, 1)

            def exps(h):
                act.wait_ge(s_less_max, h + 1)
                nc.scalar.activation(e_sb[:, h, :, :], s_sb[:, h, :, :], ACT.Exp, scale=SCALE).then_inc(e_ready, 1)

            def yT_copy(h):
                act.wait_ge(yT_psum, h + 1)
                nc.scalar.copy(y1T[:, h, :], p_yT[h]).then_inc(yT_ready, 1)

            def gate_exp(h):
                act.wait_ge(gd_ready, h + 1)
                nc.scalar.activation(tope[:, h, :, :], tope[:, h, :, :], ACT.Exp).then_inc(ge_ready, 1)

            def gT_copy(h):
                act.wait_ge(gT_psum, h + 1)
                nc.scalar.copy(gT[:, h, :], p_gT[h]).then_inc(gT_ready, 1)

            def relu(h, e):
                act.wait_ge(hid_psum, h * E + e + 1)
                nc.scalar.activation(p_hid[:, e % 4, :], p_hid[:, e % 4, :], ACT.Relu,
                                     bias=w2b1_sb[:, E * D + e:E * D + e + 1]).then_inc(hid_relu, 1)

            def deviation(h, k):
                act.wait_ge(mv_ready, mv_count(h, k))
                nc.scalar.activation(dev[:, h, k, :], mv[:, h, k, :, 1], ACT.Sqrt,
                                     bias=eps_t[:, :]).then_inc(dev_ready, 1)

            loads = []
            def table(function):
                nc.scalar.activation(loaded[:, len(loads):len(loads) + 1], eps_t[0:1, :], function)
                loads.append(function)

            def moe_copy(h):
                act.wait_ge(hid_used, (h + 1) * PAIRS)
                nc.scalar.copy(moe[:, h, :], p_moe[h]).then_inc(moe_ready, 1)

            tokens_hi(0)
            t_copy(0)
            exps(0)
            tokens_hi(1)
            table(ACT.Sqrt)
            t_copy(1)
            deviation(0, 0)
            act.wait_ge(w1_in, 32)
            nc.scalar.copy(w1_hi[:, 0:E // 2, :], w1_sb[:, 0:E // 2, :]).then_inc(w1_hi_ready, 1)
            table(ACT.Exp)
            yT_copy(0)
            exps(1)
            nc.scalar.copy(w1_hi[:, E // 2:E, :], w1_sb[:, E // 2:E, :]).then_inc(w1_hi_ready, 1)
            gate_exp(0)
            table(ACT.Sqrt)
            act.wait_ge(w2_in, 16)
            gT_copy(0)
            deviation(1, 0)
            relu(0, 0)
            relu(0, 1)
            table(ACT.Exp)
            relu(0, 2)
            relu(0, 3)
            yT_copy(1)
            for e in range(4, E):
                relu(0, e)
                if e == 5:
                    gate_exp(1)
                    table(ACT.Sqrt)
                if e == 9:
                    gT_copy(1)
            for e in range(E):
                relu(1, e)
                if e == 1:
                    moe_copy(0)
                if e == 6:
                    deviation(0, 1)
                if e == 13:
                    deviation(0, 2)
            moe_copy(1)
            deviation(1, 1)
            deviation(1, 2)

        @block.vector
        def _(dve):
            steps = [0]
            def step(ins):
                steps[0] += 1
                ins.then_inc(dve_step, 1)
                return steps[0]

            def tokens_lo(h):
                dve.wait_ge(h_hi, h + 1)
                lo = hT[D:P, h, :]
                nc.vector.scalar_tensor_tensor(out=lo, in0=p_h[h][D:P, :], scalar=tok_b[D:P, :],
                                               in1=lo.bitcast(F32), op0=ALU.add,
                                               op1=ALU.subtract).then_inc(h_lo, 1)

            def softmax_in(h):
                shape = [TT, NT, TT]
                dve.wait_ge(s_psum, h + 1)
                n = step(nc.vector.tensor_tensor(s_sb[:, h, :, :], p_s[h], bc(mask[:, :].unsqueeze(1), shape), ALU.add))
                dve.wait_ge(dve_step, n)
                n = step(nc.vector.tensor_reduce(smax[:, h, :], s_sb[:, h, :, :], AX_X, ALU.max))
                dve.wait_ge(dve_step, n)
                nc.vector.tensor_tensor(s_sb[:, h, :, :], s_sb[:, h, :, :], bc(smax[:, h, :].unsqueeze(2), shape),
                                        ALU.subtract).then_inc(s_less_max, 1)

            def softmax_sums(h):
                dve.wait_ge(e_ready, h + 1)
                n = step(nc.vector.tensor_reduce(ssum[:, h, :], e_sb[:, h, :, :], AX_X, ALU.add))
                dve.wait_ge(dve_step, n)
                return step(nc.vector.reciprocal(srec[:, h, :], ssum[:, h, :]))

            def values(h, sums_step):
                dve.wait_ge(dve_step, sums_step)
                dve.wait_ge(v_psum, h + 1)
                nc.vector.tensor_tensor(vs[:, h, :, :], p_v[h], bc(srec[:, h, :].unsqueeze(2), [TT, NT, D]),
                                        ALU.mult).then_inc(vs_ready, 1)

            def tile_stats(h, k, t, src):
                return step(nc.vector.bn_stats(stats[:, h, k, t, :], src[:, t, :]))

            def mean_variance(h, k, stats_steps):
                for t in range(NT):
                    dve.wait_ge(dve_step, stats_steps[t])
                    last = nc.vector.bn_aggr(mv[:, h, k, t, :], stats[:, h, k, t, :])
                last.then_inc(mv_ready, 1)

            def centre(h, k, src):
                return nc.vector.tensor_tensor(cen[:, h, k, :, :], src, bc(mv[:, h, k, :, 0:1], [TT, NT, D]),
                                               ALU.subtract)

            def scale(h, k, dst):
                return nc.vector.tensor_tensor(dst, cen[:, h, k, :, :],
                                               bc(rstd[:, h, k, :].unsqueeze(2), [TT, NT, D]), ALU.mult)

            def norm1(h):
                dve.wait_ge(y_psum, h + 1)
                mean_variance(h, 0, [tile_stats(h, 0, t, p_y[h]) for t in range(NT)])
                dve.wait_ge(mv_ready, mv_count(h, 0))
                step(centre(h, 0, p_y[h]))
                reciprocal_deviation(h, 0)
                dve.wait_ge(dve_step, steps[0])
                n = step(scale(h, 0, y1[:, h, :, :]))
                n = step(scale(h, 0, y1s[:, h, :, 0, :]))
                dve.wait_ge(dve_step, n)
                nc.vector.tensor_tensor(y1s[:, h, :, 1, :], y1[:, h, :, :], y1s[:, h, :, 0, :].bitcast(F32),
                                        ALU.subtract).then_inc(y1_lo, 1)

            def gates_top(h):
                dve.wait_ge(lg_psum, h + 1)
                n = step(nc.vector.tensor_tensor(lgb[:, h, :, :], p_lg[h][:, :, 0:E],
                                                 bc(gate_b.unsqueeze(1), [TT, NT, E]), ALU.add))
                dve.wait_ge(dve_step, n)
                nc.vector.tensor_tensor(lg[:, h, :, :], p_lg[h][:, :, E:2 * E], lgb[:, h, :, :],
                                        ALU.add).then_inc(lg_ready, 1)
                dve.wait_ge(lg_ready, h + 1)
                for t in range(NT):
                    n = step(nc.vector.max(top[:, h, t, :], lg[:, h, t, :]))
                dve.wait_ge(dve_step, n)
                nc.vector.tensor_tensor(tope[:, h, :, :], top[:, h, :, 0:TOPK],
                                        bc(top[:, h, :, 0:1], [TT, NT, TOPK]), ALU.subtract).then_inc(gd_ready, 1)

            def gates_places(h):
                for t in range(NT):
                    n = step(nc.vector.max_index(topi[:, h, t, :], top[:, h, t, :], lg[:, h, t, :]))
                dve.wait_ge(dve_step, n)
                shape = [TT, NT, TOPK, E]
                nc.vector.tensor_tensor(hot[:, h, :, :, :], bc(iota_e[:, :].unsqueeze(1).unsqueeze(1), shape),
                                        bc(topi[:, h, :, 0:TOPK].unsqueeze(3), shape),
                                        ALU.is_equal).then_inc(hot_ready, 1)

            def gates_out(h):
                shape = [TT, NT, TOPK, E]
                dve.wait_ge(ge_ready, h + 1)
                m = step(nc.vector.tensor_reduce(gsum[:, h, :], tope[:, h, :, :], AX_X, ALU.add))
                dve.wait_ge(hot_ready, h + 1)
                n = step(nc.vector.tensor_tensor(hot[:, h, :, :, :], hot[:, h, :, :, :],
                                                 bc(tope[:, h, :, :].unsqueeze(3), shape), ALU.mult))
                dve.wait_ge(dve_step, m)
                m = step(nc.vector.reciprocal(grec[:, h, :], gsum[:, h, :]))
                dve.wait_ge(dve_step, n)
                n = step(nc.vector.tensor_tensor(gun[:, h, :, :], hot[:, h, :, 0, :], hot[:, h, :, 1, :], ALU.add))
                dve.wait_ge(dve_step, n)
                nc.vector.tensor_tensor(g[:, h, :, :], gun[:, h, :, :],
                                        bc(grec[:, h, :].unsqueeze(2), [TT, NT, E]), ALU.mult).then_inc(g_ready, 1)

            def gate_hidden(h, e):
                i = h * E + e
                dve.wait_ge(hid_relu, i + 1)
                dve.wait_ge(gb_ready, i + 1)
                if i >= NH:
                    dve.wait_ge(hid_used, (i - NH) // 2 + 1)
                nc.vector.tensor_tensor(hid[:, i % NH, :], p_hid[:, e % 4, :], gb[:, h, e, :],
                                        ALU.mult).then_inc(hid_ready, 1)

            def norm2_stats(h):
                dve.wait_ge(fin_psum, h + 1)
                return [tile_stats(h, 1, t, p_fin[h]) for t in range(NT)]

            def norm2_gamma(h):
                dve.wait_ge(mv_ready, mv_count(h, 1))
                return [step(nc.vector.scalar_tensor_tensor(out=n2g[:, h, t, :], in0=p_fin[h][:, t, :],
                                                            scalar=mv[:, h, 1, t, 0:1], in1=gamma,
                                                            op0=ALU.subtract, op1=ALU.mult)) for t in range(NT)]

            def reciprocal_deviation(h, k):
                dve.wait_ge(dev_ready, mv_count(h, k))
                step(nc.vector.reciprocal(rstd[:, h, k, :], dev[:, h, k, :]))

            def norm2_out(h):
                dve.wait_ge(ybeta_ready, h + 1)
                dve.wait_ge(dve_step, steps[0])
                return [step(nc.vector.scalar_tensor_tensor(out=y3[:, h, t, :], in0=n2g[:, h, t, :],
                                                            scalar=rstd[:, h, 1, t:t + 1], in1=ybeta[:, h, t, :],
                                                            op0=ALU.mult, op1=ALU.add)) for t in range(NT)]

            def norm3_stats(h, y3_steps):
                done = []
                for t in range(NT):
                    dve.wait_ge(dve_step, y3_steps[t])
                    done.append(tile_stats(h, 2, t, y3[:, h, :, :]))
                return done

            def norm3_centre(h):
                dve.wait_ge(mv_ready, mv_count(h, 2))
                step(centre(h, 2, y3[:, h, :, :]))

            def norm3_out(h):
                dve.wait_ge(dve_step, steps[0])
                scale(h, 2, fin[:, h, :, :]).then_inc(fin_ready, 1)

            nc.vector.memset(zeros[:, :], 0.0).then_inc(zeros_ready, 1)
            dve.wait_ge(tokw_in, 16)
            nc.vector.tensor_copy(tokw_sb[:, :, 1, :], tokw_sb[:, :, 0, :]).then_inc(tokw_doubled, 1)
            dve.wait_ge(wvg_hi_ready, 1)
            nc.vector.tensor_tensor(wvg[:, 1, :], wvgb_sb[:, 0:D + E], wvg[:, 0, :].bitcast(F32),
                                    ALU.subtract).then_inc(wvg_lo_ready, 1)
            dve.wait_ge(a_hi_ready, 1)
            nc.vector.tensor_tensor(a_lo[:, :, :], bc(p_a.unsqueeze(1), [P, 2, D]), a_hi[:, :, :].bitcast(F32),
                                    ALU.subtract).then_inc(a_lo_ready, 1)
            dve.wait_ge(consts, 5)
            tokens_lo(0)
            softmax_in(0)
            values(0, softmax_sums(0))
            tokens_lo(1)
            norm1(0)
            softmax_in(1)
            dve.wait_ge(rows_in, 16)
            sums_step = softmax_sums(1)
            gates_top(0)
            values(1, sums_step)
            gates_places(0)
            gates_out(0)
            norm1(1)
            for e in range(E):
                gate_hidden(0, e)
                if e == 3:
                    gates_top(1)
                if e == 4:
                    gates_places(1)
                if e == 5:
                    gates_out(1)
            for e in range(E):
                gate_hidden(1, e)
                if e == 3:
                    done = norm2_stats(0)
                if e == 4:
                    mean_variance(0, 1, done)
                if e == 5:
                    norm2_gamma(0)
                if e == 7:
                    reciprocal_deviation(0, 1)
                if e == 8:
                    done = norm2_out(0)
                if e == 9:
                    done = norm3_stats(0, done)
                if e == 10:
                    mean_variance(0, 2, done)
                if e == 11:
                    norm3_centre(0)
                if e == 13:
                    reciprocal_deviation(0, 2)
                if e == 14:
                    norm3_out(0)
            mean_variance(1, 1, norm2_stats(1))
            norm2_gamma(1)
            reciprocal_deviation(1, 1)
            mean_variance(1, 2, norm3_stats(1, norm2_out(1)))
            norm3_centre(1)
            reciprocal_deviation(1, 2)
            norm3_out(1)

        @block.tensor
        def _(pe):
            def embed(h, j):
                pe.wait_ge(x_in[h][j], 16)
                for c in (2 * j, 2 * j + 1):
                    mm = nc.tensor.matmul(p_h[h], tokw_sb[:, c, :, :].rearrange("p a d -> p (a d)"), xk[:, h, c, :],
                                          start=(c == 0), stop=(c == CH - 1))
                if j == CH // 2 - 1:
                    mm.then_inc(h_psum, 1)

            def project(h):
                pe.wait_ge(h_lo, h + 1)
                nc.tensor.matmul(p_t[h], a_hi[:, :, :].rearrange("p a d -> p (a d)"), hT[:, h, :], start=True, stop=False)
                nc.tensor.matmul(p_t[h], a_lo[:, :, :].rearrange("p a d -> p (a d)"), hT[:, h, :], start=False, stop=True).then_inc(t_psum, 1)

            def scores(h):
                pe.wait_ge(t_ready, h + 1)
                for t in range(NT):
                    cols = slice(TT * t, TT * (t + 1))
                    mm = nc.tensor.matmul(p_s[h][:, t, :], hT[:, h, cols].bitcast(F32), tT[:, h, cols],
                                          start=True, stop=True)
                mm.then_inc(s_psum, 1)

            def value_rows(h):
                for t in range(NT):
                    keys = hT[:, h, TT * t:TT * (t + 1)]
                    nc.tensor.matmul(p_v[h][:, t, :], keys, wvg[:, 0, 0:D], start=True, stop=False)
                    mm = nc.tensor.matmul(p_v[h][:, t, :], keys, wvg[:, 1, 0:D], start=False, stop=True)
                mm.then_inc(v_psum, 1)

            def attend(h):
                pe.wait_ge(vs_ready, h + 1)
                for t in range(NT):
                    nc.tensor.matmul(p_y[h][:, t, :], hT[:, h, TT * t:TT * (t + 1)], ident2_r[:, :],
                                     start=True, stop=False)
                    mm = nc.tensor.matmul(p_y[h][:, t, :], e_sb[:, h, t, :], vs[:, h, t, :], start=False, stop=True)
                mm.then_inc(y_psum, 1)

            def y1_transpose(h):
                pe.wait_ge(y1_lo, h + 1)
                for t in range(NT):
                    mm = nc.tensor.transpose(p_yT[h][:, TT * t:TT * (t + 1)],
                                             y1s[:, h, t, :, :].rearrange("p a d -> p (a d)").bitcast(F32),
                                             ident[0:TT, 0:TT])
                mm.then_inc(yT_psum, 1)

            def logits(h):
                pe.wait_ge(yT_ready, h + 1)
                for t in range(NT):
                    mm = nc.tensor.matmul(p_lg[h][:, t, :].rearrange("p (a e) -> p a e", a=2),
                                          y1T[:, h, TT * t:TT * (t + 1)], wvg[:, :, D:D + E], start=True, stop=True)
                mm.then_inc(lg_psum, 1)

            def gates_transpose(h):
                pe.wait_ge(g_ready, h + 1)
                for t in range(NT):
                    mm = nc.tensor.transpose(p_gT[h][:, TT * t:TT * (t + 1)], g[:, h, t, :], ident[0:TT, 0:TT])
                mm.then_inc(gT_psum, 1)

            def expert_in(i):
                h, e = divmod(i, E)
                if i >= 4:
                    pe.wait_ge(hid_ready, i - 3)
                nc.tensor.matmul(p_hid[:, e % 4, :], w1_hi[:, e, :], y1T[:, h, :], start=True, stop=False)
                nc.tensor.matmul(p_hid[:, e % 4, :], w1_lo[:, e, :], y1T[:, h, :],
                                 start=False, stop=True).then_inc(hid_psum, 1)

            def expert_out(h, p):
                i = h * E + 2 * p
                pe.wait_ge(hid_ready, i + 2)
                for j in range(2):
                    mm = nc.tensor.matmul(p_moe[h][D * j:D * (j + 1), :], w2_sb[:, 2 * p + j, :],
                                          hid[:, (i + j) % NH, :], start=(p == 0), stop=(p == PAIRS - 1))
                mm.then_inc(hid_used, 1)

            def combine_first(h):
                for t in range(NT):
                    cols = slice(TT * t, TT * (t + 1))
                    nc.tensor.matmul(p_fin[h][:, t, :], gT[:, h, cols], b2_sb[:, :], start=(t == 0), stop=False,
                                     skip_group_check=True)
                    nc.tensor.matmul(p_fin[h][:, t, :], y1T[:, h, cols], ident2_r[:, :], start=False, stop=False,
                                     skip_group_check=True)

            def combine(h):
                pe.wait_ge(moe_ready, h + 1)
                for t in range(NT):
                    cols = slice(TT * t, TT * (t + 1))
                    mm = nc.tensor.matmul(p_fin[h][:, t, :], moe[:, h, cols], ident2[:, :], start=False, stop=True,
                                          skip_group_check=True)
                mm.then_inc(fin_psum, 1)

            def keep_warm(n):
                for _ in range(n):
                    nc.tensor.matmul(banks[:, 4, :], zeros[:, 0:P], zeros[:, :], start=True, stop=True)

            pe.wait_ge(zeros_ready, 1)
            keep_warm(WARM)
            pe.wait_ge(tokw_doubled, 1)
            embed(0, 0)
            embed(0, 1)
            embed(0, 2)
            pe.wait_ge(qk_in, 16)
            nc.tensor.matmul(p_a, qk_sb[:, 0:2 * D], qk_sb[:, 2 * D:3 * D], start=True, stop=True).then_inc(a_psum, 1)
            embed(1, 0)
            pe.wait_ge(a_hi_ready, 1)
            pe.wait_ge(a_lo_ready, 1)
            project(0)
            scores(0)
            pe.wait_ge(wvg_lo_ready, 1)
            value_rows(0)
            embed(1, 1)
            embed(1, 2)
            pe.wait_ge(ident2_r_ready, 1)
            attend(0)
            project(1)
            scores(1)
            value_rows(1)
            pe.wait_ge(consts, 5)
            keep_warm(K1)
            y1_transpose(0)
            keep_warm(K2)
            logits(0)
            pe.wait_ge(w1_lo_ready, 1)
            expert_in(0)
            expert_in(1)
            keep_warm(K0)
            attend(1)
            keep_warm(K3)
            gates_transpose(0)
            pe.wait_ge(gT_ready, 1)
            expert_in(2)
            expert_in(3)
            keep_warm(K4)
            pe.wait_ge(w1_lo_ready, 2)
            pe.wait_ge(w2_in, 16)
            pe.wait_ge(b2_in, 16)
            y1_transpose(1)
            keep_warm(K2)
            logits(1)
            for p in range(PAIRS):
                expert_in(2 * p + 4)
                expert_in(2 * p + 5)
                expert_out(0, p)
                if p == 1:
                    combine_first(0)
                if p == 3:
                    gates_transpose(1)
            pe.wait_ge(gT_ready, 2)
            for p in range(PAIRS):
                if p + 2 < PAIRS:
                    expert_in(E + 2 * p + 4)
                    expert_in(E + 2 * p + 5)
                expert_out(1, p)
                if p == 0:
                    combine(0)
                if p == 1:
                    combine_first(1)
            combine(1)


def kernel(**inputs):
    import numpy as np
    import concourse.bacc as bacc
    from concourse.bass_utils import run_bass_kernel_spmd

    a = {k: np.asarray(v) for k, v in inputs.items()}
    x = a["x"]
    B, C, H, W = x.shape
    nh, nw = H // PATCH, W // PATCH
    D, K = a["L0_tok_W"].shape
    E, _, F = a["L0_ffn_w1"].shape
    tokens = B * nh * nw
    ch = K // 128
    xt = x.reshape(B, C, nh, PATCH, nw, PATCH).transpose(1, 3, 5, 0, 2, 4).reshape(ch, 128, 2, tokens // 2)
    arrays = {
        "x_kt": xt.transpose(1, 2, 0, 3),
        "tokw": a["L0_tok_W"].T.reshape(ch, 128, D).transpose(1, 0, 2),
        "qk": np.concatenate([a["L0_attn_Wq"], a["L0_attn_Wq"], a["L0_attn_Wk"]], axis=1),
        "wvgb": np.concatenate([a["L0_attn_Wv"].T, a["L0_ffn_gate_w"], a["L0_tok_b"][:, None]], axis=1),
        "w1": a["L0_ffn_w1"].transpose(1, 0, 2),
        "w2b1": np.concatenate([a["L0_ffn_w2"].transpose(1, 0, 2).reshape(F, E * D), a["L0_ffn_b1"].T], axis=1),
        "b2": a["L0_ffn_b2"],
        "rows": np.concatenate([a["L0_ffn_gate_b"], a["L0_ffn_gamma"], a["L0_ffn_beta"]]),
    }
    arrays = {k: np.ascontiguousarray(v) for k, v in arrays.items()}
    nc = bacc.Bacc("TRN2", target_bir_lowering=False, num_devices=1)
    args = [nc.dram_tensor(k, v.shape, mybir.dt.from_np(v.dtype), kind="ExternalInput").ap()
            for k, v in arrays.items()]
    out = nc.dram_tensor("out", (B, nh * nw, D), F32, kind="ExternalOutput").ap()
    vit_tower(nc, *args, out)
    r = run_bass_kernel_spmd(nc, [arrays], core_ids=[0])
    return r.results[0]["out"]
```

```python
from contextlib import ExitStack

import concourse.bass as bass
from concourse import mybir

F32 = mybir.dt.float32
F32R = mybir.dt.float32r
U32 = mybir.dt.uint32
ALU = mybir.AluOpType
ACT = mybir.ActivationFunctionType
AX_X = mybir.AxisListType.X

PATCH = 16
TOPK = 2
WARM = 8
WARM_VALUES, WARM_NORM, WARM_COPY, WARM_GATES, WARM_NORM_1 = 9, 4, 2, 2, 4
EPS = 1e-5
MASKED = -1.0e10
OTHER_IMAGE = -1.0e30


def vit_tower(nc: bass.Bass, x_kt, tokw, qk, wvgb, w1, w2b1, b2, rows, out):
    P, HALVES, CH, HT = x_kt.shape
    D = tokw.shape[2]
    E, F = w1.shape[1], w1.shape[2]
    N = out.shape[1]
    TT = 2 * N
    NT = HT // TT
    PAIRS = E // 2
    SCALE = float(D) ** -0.5
    assert P == 2 * D == F and NT * TT == HT and out.shape[0] * N == HALVES * HT

    with ExitStack() as ctx:
        def sb(name, shape, dt=F32):
            return ctx.enter_context(nc.sbuf_tensor(name, shape, dt))

        def sem(name):
            return ctx.enter_context(nc.semaphore(name))

        xk = sb("xk", [P, HALVES, CH, HT])
        tokw_sb = sb("tokw_sb", [P, CH, 2, D])
        qk_sb = sb("qk_sb", [D, 3 * D])
        wvgb_sb = sb("wvgb_sb", [P, D + E + 1])
        w1_sb = sb("w1_sb", [P, E, F])
        w2b1_sb = sb("w2b1_sb", [F, E * D + E])
        b2_sb = sb("b2_sb", [E, D])
        rows_sb = sb("rows_sb", [TT, E + 2 * D])
        w2_sb = w2b1_sb[:, 0:E * D].rearrange("f (e d) -> f e d", e=E)
        tok_b = wvgb_sb[:, D + E:D + E + 1]
        gate_b, gamma, beta = rows_sb[:, 0:E], rows_sb[:, E:E + D], rows_sb[:, E + D:E + 2 * D]

        ident = sb("ident", [P, P])
        ident2 = sb("ident2", [P, D])
        ident2_r = sb("ident2_r", [P, D], F32R)
        mask = sb("mask", [TT, TT])
        iota_e = sb("iota_e", [TT, E])

        a_hi = sb("a_hi", [P, 2, D], F32R)
        a_lo = sb("a_lo", [P, 2, D], F32R)
        wvg = sb("wvg", [P, 2, D + E], F32R)
        w1_hi = sb("w1_hi", [P, E, F], F32R)
        w1_lo = sb("w1_lo", [P, E, F], F32R)

        hT = sb("hT", [P, HALVES, HT], F32R)
        tT = sb("tT", [P, HALVES, HT])
        s_sb = sb("s_sb", [TT, HALVES, NT, TT])
        e_sb = sb("e_sb", [TT, HALVES, NT, TT])
        smax = sb("smax", [TT, HALVES, NT])
        ssum = sb("ssum", [TT, HALVES, NT])
        srec = sb("srec", [TT, HALVES, NT])
        vs = sb("vs", [TT, HALVES, NT, D])
        y1 = sb("y1", [TT, HALVES, NT, D])
        y1s = sb("y1s", [TT, HALVES, NT, 2, D], F32R)
        y1T = sb("y1T", [P, HALVES, HT], F32R)
        lg = sb("lg", [TT, HALVES, NT, E])
        top = sb("top", [TT, HALVES, NT, 8])
        topi = sb("topi", [TT, HALVES, NT, 8], U32)
        lgb = sb("lgb", [TT, HALVES, NT, E])
        tope = sb("tope", [TT, HALVES, NT, TOPK])
        gsum = sb("gsum", [TT, HALVES, NT])
        grec = sb("grec", [TT, HALVES, NT])
        hot = sb("hot", [TT, HALVES, NT, TOPK, E])
        gun = sb("gun", [TT, HALVES, NT, E])
        g = sb("g", [TT, HALVES, NT, E])
        gT = sb("gT", [E, HALVES, HT])
        grow = sb("grow", [1, HALVES, E * HT])
        gb = sb("gb", [P, HALVES, E, HT])
        NH = 6
        hid = sb("hid", [F, NH, HT])
        moe = sb("moe", [P, HALVES, HT])
        ybeta = sb("ybeta", [TT, HALVES, NT, D])
        stats = sb("stats", [TT, HALVES, 3, NT, 6])
        mv = sb("mv", [TT, HALVES, 3, NT, 2])
        rstd = sb("rstd", [TT, HALVES, 3, NT])
        dev = sb("dev", [TT, HALVES, 3, NT])
        eps_t = sb("eps_t", [TT, 1])
        zeros = sb("zeros", [P, 512], mybir.dt.bfloat16)
        loaded = sb("loaded", [1, 8])
        bwarm = sb("bwarm", [P, 8])
        eps_row = sb("eps_row", [1, 8])
        cen = sb("cen", [TT, HALVES, 3, NT, D])
        n2g = sb("n2g", [TT, HALVES, NT, D])
        y3 = sb("y3", [TT, HALVES, NT, D])
        fin = sb("fin", [TT, HALVES, NT, D])

        banks = ctx.enter_context(nc.psum_tensor("banks", [P, 8, 512], F32))

        def tok_tiles(bank, width):
            return banks[0:TT, bank, 0:NT * width].rearrange("p (t d) -> p t d", t=NT)

        p_a = banks[:, 4, 0:D]
        p_h = [banks[:, b, 0:HT] for b in (0, 5)]
        p_t = [banks[:, b, 0:HT] for b in (1, 6)]
        p_s = [tok_tiles(b, TT) for b in (2, 7)]
        p_v = [tok_tiles(b, D) for b in (3, 5)]
        p_y = [tok_tiles(b, D) for b in (0, 6)]
        p_yT = [banks[:, b, 0:HT] for b in (1, 6)]
        p_lg = [tok_tiles(b, 2 * E) for b in (2, 5)]
        p_gT = [banks[0:E, b, 0:HT] for b in (3, 6)]
        p_moe = [banks[:, b, 0:HT] for b in (4, 5)]
        p_fin = [tok_tiles(b, D) for b in (7, 6)]
        p_hid = banks[:, 0:4, 0:HT]

        X_PARTS = ((0, 2), (2, 4), (4, 5), (5, CH))

        x_in = [[sem(f"x_in{h}{c}") for c in range(len(X_PARTS))] for h in range(HALVES)]
        tokw_in, qk_in, wvgb_in, w1_in, w2_in, b2_in, rows_in = (
            sem(n) for n in ("tokw_in", "qk_in", "wvgb_in", "w1_in", "w2_in", "b2_in", "rows_in"))
        pool_step, consts = sem("pool_step"), sem("consts")
        ident2_r_ready = sem("ident2_r_ready")
        a_psum, a_hi_ready, a_lo_ready = sem("a_psum"), sem("a_hi_ready"), sem("a_lo_ready")
        wvg_hi_ready, wvg_lo_ready = sem("wvg_hi_ready"), sem("wvg_lo_ready")
        w1_hi_ready, w1_lo_ready = sem("w1_hi_ready"), sem("w1_lo_ready")
        h_psum, h_hi, h_lo = sem("h_psum"), sem("h_hi"), sem("h_lo")
        t_psum, t_ready = sem("t_psum"), sem("t_ready")
        s_psum, s_less_max, e_ready = sem("s_psum"), sem("s_less_max"), sem("e_ready")
        v_psum, vs_ready, y_psum = sem("v_psum"), sem("vs_ready"), sem("y_psum")
        y1_lo = sem("y1_lo")
        yT_psum, yT_ready = sem("yT_psum"), sem("yT_ready")
        lg_psum, lg_ready, gd_ready, ge_ready = sem("lg_psum"), sem("lg_ready"), sem("gd_ready"), sem("ge_ready")
        lgb_ready, hot_ready = sem("lgb_ready"), sem("hot_ready")
        g_ready, gT_psum, gT_ready = sem("g_ready"), sem("gT_psum"), sem("gT_ready")
        grow_in = [sem(f"grow_in{h}") for h in range(HALVES)]
        gb_ready = sem("gb_ready")
        hid_psum, hid_relu, hid_ready, hid_used = sem("hid_psum"), sem("hid_relu"), sem("hid_ready"), sem("hid_used")
        moe_ready, fin_psum = sem("moe_ready"), sem("fin_psum")
        fin_ready = [sem(f"fin_ready{h}") for h in range(HALVES)]
        dve_step = sem("dve_step")
        ybeta_ready, centred, recip_ready, y3_ready = (
            sem(n) for n in ("ybeta_ready", "centred", "recip_ready", "y3_ready"))
        mv_ready, dev_ready = sem("mv_ready"), sem("dev_ready")
        zeros_ready, tokw_doubled = sem("zeros_ready"), sem("tokw_doubled")
        out_done = sem("out_done")

        SUMMED = PAIRS - 1
        BCASTS = (0, 2, 4, 8, 12, E)
        out_v = out.rearrange("b n d -> (b n) d").rearrange("(h t p) d -> h p t d", h=HALVES, t=NT)

        TWO = (slice(0, NT // 2), slice(NT // 2, NT))

        def bc(ap, shape):
            return ap.to_broadcast(shape)

        def mv_count(h, k):
            return h + 1 if k == 0 else HALVES + 2 * h + k

        block = ctx.enter_context(nc.Block())

        @block.sync
        def _(sp):
            sp.dma_start(tokw_sb[:, :, 0, :], tokw).then_inc(tokw_in, 16)
            for h in range(HALVES):
                for j, (c0, c1) in enumerate(X_PARTS):
                    sp.dma_start(xk[:, h, c0:c1, :], x_kt[:, h, c0:c1, :]).then_inc(x_in[h][j], 16)
                if h == 0:
                    for r in range(2):
                        sp.dma_start(wvgb_sb[D * r:D * (r + 1), :], wvgb).then_inc(wvgb_in, 16)
            for r in range(2):
                sp.dma_start(w1_sb[D * r:D * (r + 1), :, :], w1).then_inc(w1_in, 16)
            sp.dma_start(rows_sb[:, :], rows.partition_broadcast(TT)).then_inc(rows_in, 16)
            sp.dma_start(w2b1_sb[:, :], w2b1).then_inc(w2_in, 16)
            sp.dma_start(b2_sb[:, :], b2).then_inc(b2_in, 16)
            for h in range(HALVES):
                sp.wait_ge(gT_ready, h + 1)
                sp.dma_start(grow[0:1, h, :].rearrange("o (e n) -> o e n", e=E),
                             gT[:, h, :]).then_inc(grow_in[h], 16)
            for h in range(HALVES):
                sp.wait_ge(fin_ready[h], 1)
                sp.dma_start(out_v[h], fin[:, h, :, :]).then_inc(out_done, 16)
            sp.wait_ge(out_done, 16 * HALVES)

        @block.gpsimd
        def _(pool):
            nc.gpsimd.memset(ident[:, :], 0.0).then_inc(pool_step, 1)
            nc.gpsimd.memset(ident2[:, :], 0.0).then_inc(pool_step, 1)
            nc.gpsimd.memset(mask[:, :], 0.0).then_inc(pool_step, 1)
            nc.gpsimd.memset(eps_row[:, :], EPS).then_inc(pool_step, 1)
            nc.gpsimd.memset(eps_t[:, :], EPS).then_inc(pool_step, 1)
            nc.gpsimd.iota(iota_e[:, :], pattern=[[1, E]], base=0, channel_multiplier=0,
                           allow_small_or_imprecise_dtypes=True).then_inc(consts, 1)
            pool.wait_ge(pool_step, 5)
            nc.gpsimd.affine_select(out=ident[:, :], in_=ident[:, :], compare_op=ALU.not_equal, fill=1.0,
                                    base=0, pattern=[[-1, P]], channel_multiplier=1).then_inc(consts, 1)
            nc.gpsimd.affine_select(out=ident2[:, :], in_=ident2[:, :], compare_op=ALU.not_equal, fill=1.0,
                                    base=0, pattern=[[-1, D]], channel_multiplier=1).then_inc(pool_step, 1)
            nc.gpsimd.affine_select(out=mask[:, :], in_=mask[:, :], compare_op=ALU.is_gt, fill=MASKED,
                                    base=0, pattern=[[-1, TT]], channel_multiplier=1).then_inc(pool_step, 1)
            pool.wait_ge(pool_step, 7)
            nc.gpsimd.affine_select(out=ident2[:, :], in_=ident2[:, :], compare_op=ALU.not_equal, fill=1.0,
                                    base=-D, pattern=[[-1, D]], channel_multiplier=1).then_inc(consts, 1)
            nc.gpsimd.affine_select(out=mask[:, 0:N], in_=mask[:, 0:N], compare_op=ALU.is_ge, fill=OTHER_IMAGE,
                                    base=N - 1, pattern=[[0, N]], channel_multiplier=-1).then_inc(consts, 1)
            nc.gpsimd.affine_select(out=mask[:, N:TT], in_=mask[:, N:TT], compare_op=ALU.is_ge, fill=OTHER_IMAGE,
                                    base=-N, pattern=[[0, N]], channel_multiplier=1).then_inc(consts, 1)
            nc.gpsimd.partition_broadcast(bwarm[:, :], eps_row[0:1, :], P).then_inc(pool_step, 1)
            pool.wait_ge(w1_in, 32)
            for k in range(2):
                es = slice(E // 2 * k, E // 2 * (k + 1))
                nc.gpsimd.tensor_copy(w1_hi[:, es, :], w1_sb[:, es, :]).then_inc(w1_hi_ready, 1)
                pool.wait_ge(w1_hi_ready, k + 1)
                nc.gpsimd.tensor_tensor(w1_lo[:, es, :], w1_sb[:, es, :], w1_hi[:, es, :].bitcast(F32),
                                        ALU.subtract).then_inc(w1_lo_ready, 1)
            for h in range(HALVES):
                pool.wait_ge(grow_in[h], 16)
                for e0, e1 in zip(BCASTS, BCASTS[1:]):
                    nc.gpsimd.partition_broadcast(
                        gb[:, h, e0:e1, :].rearrange("p e n -> p (e n)"),
                        grow[0:1, h, HT * e0:HT * e1], P).then_inc(gb_ready, e1 - e0)
                if h == 0:
                    pool.wait_ge(rows_in, 16)
                pool.wait_ge(y1_lo, h + 1)
                nc.gpsimd.tensor_tensor(ybeta[:, h, :, :], y1[:, h, :, :], bc(beta.unsqueeze(1), [TT, NT, D]),
                                        ALU.add).then_inc(ybeta_ready, 1)
            shape = [TT, NT, D]
            pool.wait_ge(centred, 1)
            nc.gpsimd.tensor_tensor(n2g[:, 0, :, :], cen[:, 0, 1, :, :], bc(gamma.unsqueeze(1), shape),
                                    ALU.mult).then_inc(pool_step, 1)
            pool.wait_ge(pool_step, 9)
            pool.wait_ge(recip_ready, 1)
            nc.gpsimd.tensor_tensor(n2g[:, 0, :, :], n2g[:, 0, :, :], bc(rstd[:, 0, 1, :].unsqueeze(2), shape),
                                    ALU.mult).then_inc(pool_step, 1)
            pool.wait_ge(pool_step, 10)
            pool.wait_ge(ybeta_ready, 1)
            nc.gpsimd.tensor_tensor(y3[:, 0, :, :], n2g[:, 0, :, :], ybeta[:, 0, :, :], ALU.add).then_inc(y3_ready, 1)
            pool.wait_ge(mv_ready, mv_count(0, 2))
            nc.gpsimd.tensor_tensor(cen[:, 0, 2, :, :], y3[:, 0, :, :], bc(mv[:, 0, 2, :, 0:1], shape),
                                    ALU.subtract).then_inc(pool_step, 1)
            pool.wait_ge(pool_step, 11)
            pool.wait_ge(recip_ready, 2)
            nc.gpsimd.tensor_tensor(fin[:, 0, :, :], cen[:, 0, 2, :, :], bc(rstd[:, 0, 2, :].unsqueeze(2), shape),
                                    ALU.mult).then_inc(fin_ready[0], 1)

        @block.scalar
        def _(act):
            act.dma_start(qk_sb[:, :], qk).then_inc(qk_in, 16)
            act.wait_ge(consts, 5)
            nc.scalar.copy(ident2_r[:, :], ident2[:, :]).then_inc(ident2_r_ready, 1)
            act.wait_ge(a_psum, 1)
            nc.scalar.copy(a_hi[:, :, :], bc(p_a.unsqueeze(1), [P, 2, D])).then_inc(a_hi_ready, 1)
            act.wait_ge(wvgb_in, 32)
            nc.scalar.copy(wvg[:, 0, :], wvgb_sb[:, 0:D + E]).then_inc(wvg_hi_ready, 1)

            def tokens_hi(h):
                act.wait_ge(h_psum, h + 1)
                nc.scalar.activation(hT[:, h, :], p_h[h], ACT.Identity, bias=tok_b).then_inc(h_hi, 1)

            def t_copy(h):
                act.wait_ge(t_psum, h + 1)
                nc.scalar.copy(tT[:, h, :], p_t[h]).then_inc(t_ready, 1)

            def exps(h):
                for k, ts in enumerate(TWO):
                    act.wait_ge(s_less_max, 2 * h + k + 1)
                    nc.scalar.activation(e_sb[:, h, ts, :], s_sb[:, h, ts, :], ACT.Exp, scale=SCALE).then_inc(e_ready, 1)

            def yT_copy(h):
                act.wait_ge(yT_psum, h + 1)
                nc.scalar.copy(y1T[:, h, :], p_yT[h]).then_inc(yT_ready, 1)

            def gate_exp(h):
                act.wait_ge(gd_ready, h + 1)
                nc.scalar.activation(tope[:, h, :, :], tope[:, h, :, :], ACT.Exp).then_inc(ge_ready, 1)

            def gT_copy(h):
                act.wait_ge(gT_psum, h + 1)
                nc.scalar.copy(gT[:, h, :], p_gT[h]).then_inc(gT_ready, 1)

            def relu(h, e):
                act.wait_ge(hid_psum, h * E + e + 1)
                nc.scalar.activation(p_hid[:, e % 4, :], p_hid[:, e % 4, :], ACT.Relu,
                                     bias=w2b1_sb[:, E * D + e:E * D + e + 1]).then_inc(hid_relu, 1)

            def deviation(h, k):
                act.wait_ge(mv_ready, mv_count(h, k))
                nc.scalar.activation(dev[:, h, k, :], mv[:, h, k, :, 1], ACT.Sqrt,
                                     bias=eps_t[:, :]).then_inc(dev_ready, 1)

            loads = []
            def table(function):
                nc.scalar.activation(loaded[:, len(loads):len(loads) + 1], eps_t[0:1, :], function)
                loads.append(function)

            def moe_copy(h):
                act.wait_ge(hid_used, PAIRS if h == 0 else PAIRS + SUMMED)
                nc.scalar.copy(moe[:, h, :], p_moe[h]).then_inc(moe_ready, 1)

            tokens_hi(0)
            t_copy(0)
            exps(0)
            tokens_hi(1)
            table(ACT.Sqrt)
            t_copy(1)
            deviation(0, 0)
            table(ACT.Exp)
            yT_copy(0)
            exps(1)
            gate_exp(0)
            table(ACT.Sqrt)
            act.wait_ge(w2_in, 16)
            gT_copy(0)
            deviation(1, 0)
            relu(0, 0)
            relu(0, 1)
            table(ACT.Exp)
            relu(0, 2)
            relu(0, 3)
            yT_copy(1)
            for e in range(4, E):
                relu(0, e)
                if e == 5:
                    gate_exp(1)
                    table(ACT.Sqrt)
                if e == 8:
                    gT_copy(1)
            for e in range(E):
                relu(1, e)
                if e == 1:
                    moe_copy(0)
                if e == 6:
                    deviation(0, 1)
            moe_copy(1)
            deviation(0, 2)
            deviation(1, 1)
            deviation(1, 2)

        @block.vector
        def _(dve):
            steps = [0]
            def step(ins):
                steps[0] += 1
                ins.then_inc(dve_step, 1)
                return steps[0]

            def tokens_lo(h):
                dve.wait_ge(h_hi, h + 1)
                lo = hT[D:P, h, :]
                nc.vector.scalar_tensor_tensor(out=lo, in0=p_h[h][D:P, :], scalar=tok_b[D:P, :],
                                               in1=lo.bitcast(F32), op0=ALU.add,
                                               op1=ALU.subtract).then_inc(h_lo, 1)

            def softmax_in(h):
                shape = [TT, NT // 2, TT]
                dve.wait_ge(s_psum, h + 1)
                masked = [step(nc.vector.tensor_tensor(s_sb[:, h, ts, :], p_s[h][:, ts, :],
                                                       bc(mask[:, :].unsqueeze(1), shape), ALU.add)) for ts in TWO]
                tops = []
                for k, ts in enumerate(TWO):
                    dve.wait_ge(dve_step, masked[k])
                    tops.append(step(nc.vector.tensor_reduce(smax[:, h, ts], s_sb[:, h, ts, :], AX_X, ALU.max)))
                for k, ts in enumerate(TWO):
                    dve.wait_ge(dve_step, tops[k])
                    nc.vector.tensor_tensor(s_sb[:, h, ts, :], s_sb[:, h, ts, :], bc(smax[:, h, ts].unsqueeze(2), shape),
                                            ALU.subtract).then_inc(s_less_max, 1)

            def softmax_sums(h):
                for k, ts in enumerate(TWO):
                    dve.wait_ge(e_ready, 2 * h + k + 1)
                    n = step(nc.vector.tensor_reduce(ssum[:, h, ts], e_sb[:, h, ts, :], AX_X, ALU.add))
                dve.wait_ge(dve_step, n)
                return step(nc.vector.reciprocal(srec[:, h, :], ssum[:, h, :]))

            def values(h, sums_step):
                dve.wait_ge(dve_step, sums_step)
                dve.wait_ge(v_psum, h + 1)
                nc.vector.tensor_tensor(vs[:, h, :, :], p_v[h], bc(srec[:, h, :].unsqueeze(2), [TT, NT, D]),
                                        ALU.mult).then_inc(vs_ready, 1)

            def tile_stats(h, k, t, src):
                return step(nc.vector.bn_stats(stats[:, h, k, t, :], src[:, t, :]))

            def mean_variance(h, k, stats_steps):
                for t in range(NT):
                    dve.wait_ge(dve_step, stats_steps[t])
                    last = nc.vector.bn_aggr(mv[:, h, k, t, :], stats[:, h, k, t, :])
                last.then_inc(mv_ready, 1)

            def centre(h, k, src):
                return nc.vector.tensor_tensor(cen[:, h, k, :, :], src, bc(mv[:, h, k, :, 0:1], [TT, NT, D]),
                                               ALU.subtract)

            def scale(h, k, dst):
                return nc.vector.tensor_tensor(dst, cen[:, h, k, :, :],
                                               bc(rstd[:, h, k, :].unsqueeze(2), [TT, NT, D]), ALU.mult)

            def norm1(h):
                dve.wait_ge(y_psum, h + 1)
                mean_variance(h, 0, [tile_stats(h, 0, t, p_y[h]) for t in range(NT)])
                dve.wait_ge(mv_ready, mv_count(h, 0))
                step(centre(h, 0, p_y[h]))
                reciprocal_deviation(h, 0)
                dve.wait_ge(dve_step, steps[0])
                n = step(scale(h, 0, y1[:, h, :, :]))
                n = step(scale(h, 0, y1s[:, h, :, 0, :]))
                dve.wait_ge(dve_step, n)
                nc.vector.tensor_tensor(y1s[:, h, :, 1, :], y1[:, h, :, :], y1s[:, h, :, 0, :].bitcast(F32),
                                        ALU.subtract).then_inc(y1_lo, 1)

            def gates_bias(h):
                dve.wait_ge(lg_psum, h + 1)
                nc.vector.tensor_tensor(lgb[:, h, :, :], p_lg[h][:, :, 0:E],
                                        bc(gate_b.unsqueeze(1), [TT, NT, E]), ALU.add).then_inc(lgb_ready, 1)

            def gates_top(h):
                dve.wait_ge(lgb_ready, h + 1)
                nc.vector.tensor_tensor(lg[:, h, :, :], p_lg[h][:, :, E:2 * E], lgb[:, h, :, :],
                                        ALU.add).then_inc(lg_ready, 1)
                dve.wait_ge(lg_ready, h + 1)
                for t in range(NT):
                    n = step(nc.vector.max(top[:, h, t, :], lg[:, h, t, :]))
                dve.wait_ge(dve_step, n)
                nc.vector.tensor_tensor(tope[:, h, :, :], top[:, h, :, 0:TOPK],
                                        bc(top[:, h, :, 0:1], [TT, NT, TOPK]), ALU.subtract).then_inc(gd_ready, 1)

            def gates_places(h):
                for t in range(NT):
                    n = step(nc.vector.max_index(topi[:, h, t, :], top[:, h, t, :], lg[:, h, t, :]))
                dve.wait_ge(dve_step, n)
                shape = [TT, NT, TOPK, E]
                nc.vector.tensor_tensor(hot[:, h, :, :, :], bc(iota_e[:, :].unsqueeze(1).unsqueeze(1), shape),
                                        bc(topi[:, h, :, 0:TOPK].unsqueeze(3), shape),
                                        ALU.is_equal).then_inc(hot_ready, 1)

            def gates_out(h):
                shape = [TT, NT, TOPK, E]
                dve.wait_ge(ge_ready, h + 1)
                m = step(nc.vector.tensor_reduce(gsum[:, h, :], tope[:, h, :, :], AX_X, ALU.add))
                dve.wait_ge(hot_ready, h + 1)
                n = step(nc.vector.tensor_tensor(hot[:, h, :, :, :], hot[:, h, :, :, :],
                                                 bc(tope[:, h, :, :].unsqueeze(3), shape), ALU.mult))
                dve.wait_ge(dve_step, m)
                m = step(nc.vector.reciprocal(grec[:, h, :], gsum[:, h, :]))
                dve.wait_ge(dve_step, n)
                n = step(nc.vector.tensor_tensor(gun[:, h, :, :], hot[:, h, :, 0, :], hot[:, h, :, 1, :], ALU.add))
                dve.wait_ge(dve_step, n)
                nc.vector.tensor_tensor(g[:, h, :, :], gun[:, h, :, :],
                                        bc(grec[:, h, :].unsqueeze(2), [TT, NT, E]), ALU.mult).then_inc(g_ready, 1)

            def gate_hidden(h, e):
                i = h * E + e
                dve.wait_ge(hid_relu, i + 1)
                dve.wait_ge(gb_ready, i + 1)
                if i >= NH:
                    dve.wait_ge(hid_used, (i - NH) // 2 + 1)
                nc.vector.tensor_tensor(hid[:, i % NH, :], p_hid[:, e % 4, :], gb[:, h, e, :],
                                        ALU.mult).then_inc(hid_ready, 1)

            def norm2_stats(h):
                dve.wait_ge(fin_psum, h + 1)
                return [tile_stats(h, 1, t, p_fin[h]) for t in range(NT)]

            def norm2_gamma(h):
                dve.wait_ge(mv_ready, mv_count(h, 1))
                return [step(nc.vector.scalar_tensor_tensor(out=n2g[:, h, t, :], in0=p_fin[h][:, t, :],
                                                            scalar=mv[:, h, 1, t, 0:1], in1=gamma,
                                                            op0=ALU.subtract, op1=ALU.mult)) for t in range(NT)]

            def reciprocal_deviation(h, k):
                dve.wait_ge(dev_ready, mv_count(h, k))
                step(nc.vector.reciprocal(rstd[:, h, k, :], dev[:, h, k, :]))

            def norm2_out(h):
                dve.wait_ge(ybeta_ready, h + 1)
                dve.wait_ge(dve_step, steps[0])
                return [step(nc.vector.scalar_tensor_tensor(out=y3[:, h, t, :], in0=n2g[:, h, t, :],
                                                            scalar=rstd[:, h, 1, t:t + 1], in1=ybeta[:, h, t, :],
                                                            op0=ALU.mult, op1=ALU.add)) for t in range(NT)]

            def norm3_stats(h, y3_steps):
                done = []
                for t in range(NT):
                    dve.wait_ge(dve_step, y3_steps[t])
                    done.append(tile_stats(h, 2, t, y3[:, h, :, :]))
                return done

            def norm3_centre(h):
                dve.wait_ge(mv_ready, mv_count(h, 2))
                step(centre(h, 2, y3[:, h, :, :]))

            def norm3_out(h):
                dve.wait_ge(dve_step, steps[0])
                scale(h, 2, fin[:, h, :, :]).then_inc(fin_ready[h], 1)

            nc.vector.memset(zeros[:, :], 0.0).then_inc(zeros_ready, 1)
            dve.wait_ge(tokw_in, 16)
            nc.vector.tensor_copy(tokw_sb[:, :, 1, :], tokw_sb[:, :, 0, :]).then_inc(tokw_doubled, 1)
            dve.wait_ge(a_hi_ready, 1)
            nc.vector.tensor_tensor(a_lo[:, :, :], bc(p_a.unsqueeze(1), [P, 2, D]), a_hi[:, :, :].bitcast(F32),
                                    ALU.subtract).then_inc(a_lo_ready, 1)
            dve.wait_ge(wvg_hi_ready, 1)
            nc.vector.tensor_tensor(wvg[:, 1, :], wvgb_sb[:, 0:D + E], wvg[:, 0, :].bitcast(F32),
                                    ALU.subtract).then_inc(wvg_lo_ready, 1)
            dve.wait_ge(consts, 5)
            tokens_lo(0)
            softmax_in(0)
            values(0, softmax_sums(0))
            tokens_lo(1)
            norm1(0)
            softmax_in(1)
            dve.wait_ge(rows_in, 16)
            gates_bias(0)
            sums_step = softmax_sums(1)
            gates_top(0)
            values(1, sums_step)
            gates_places(0)
            gates_out(0)
            norm1(1)
            for e in range(E):
                gate_hidden(0, e)
                if e == 3:
                    gates_bias(1)
                    gates_top(1)
                if e == 4:
                    gates_places(1)
                if e == 5:
                    gates_out(1)
            for e in range(E):
                gate_hidden(1, e)
                if e == 3:
                    done = norm2_stats(0)
                if e == 4:
                    mean_variance(0, 1, done)
                if e == 5:
                    dve.wait_ge(mv_ready, mv_count(0, 1))
                    centre(0, 1, p_fin[0]).then_inc(centred, 1)
                if e == 7:
                    dve.wait_ge(dev_ready, mv_count(0, 1))
                    nc.vector.reciprocal(rstd[:, 0, 1, :], dev[:, 0, 1, :]).then_inc(recip_ready, 1)
            dve.wait_ge(y3_ready, 1)
            mean_variance(0, 2, [tile_stats(0, 2, t, y3[:, 0, :, :]) for t in range(NT)])
            dve.wait_ge(dev_ready, mv_count(0, 2))
            nc.vector.reciprocal(rstd[:, 0, 2, :], dev[:, 0, 2, :]).then_inc(recip_ready, 1)
            mean_variance(1, 1, norm2_stats(1))
            norm2_gamma(1)
            reciprocal_deviation(1, 1)
            mean_variance(1, 2, norm3_stats(1, norm2_out(1)))
            norm3_centre(1)
            reciprocal_deviation(1, 2)
            norm3_out(1)

        @block.tensor
        def _(pe):
            def embed(h, j):
                pe.wait_ge(x_in[h][j], 16)
                for c in range(*X_PARTS[j]):
                    mm = nc.tensor.matmul(p_h[h], tokw_sb[:, c, :, :].rearrange("p a d -> p (a d)"), xk[:, h, c, :],
                                          start=(c == 0), stop=(c == CH - 1))
                if j == len(X_PARTS) - 1:
                    mm.then_inc(h_psum, 1)

            def project(h):
                pe.wait_ge(h_lo, h + 1)
                nc.tensor.matmul(p_t[h], a_hi[:, :, :].rearrange("p a d -> p (a d)"), hT[:, h, :], start=True, stop=False)
                nc.tensor.matmul(p_t[h], a_lo[:, :, :].rearrange("p a d -> p (a d)"), hT[:, h, :], start=False, stop=True).then_inc(t_psum, 1)

            def scores(h):
                pe.wait_ge(t_ready, h + 1)
                for t in range(NT):
                    cols = slice(TT * t, TT * (t + 1))
                    mm = nc.tensor.matmul(p_s[h][:, t, :], hT[:, h, cols].bitcast(F32), tT[:, h, cols],
                                          start=True, stop=True)
                mm.then_inc(s_psum, 1)

            def value_rows(h):
                for t in range(NT):
                    keys = hT[:, h, TT * t:TT * (t + 1)]
                    nc.tensor.matmul(p_v[h][:, t, :], keys, wvg[:, 0, 0:D], start=True, stop=False)
                    mm = nc.tensor.matmul(p_v[h][:, t, :], keys, wvg[:, 1, 0:D], start=False, stop=True)
                mm.then_inc(v_psum, 1)

            def attend(h):
                pe.wait_ge(vs_ready, h + 1)
                for t in range(NT):
                    nc.tensor.matmul(p_y[h][:, t, :], hT[:, h, TT * t:TT * (t + 1)], ident2_r[:, :],
                                     start=True, stop=False)
                    mm = nc.tensor.matmul(p_y[h][:, t, :], e_sb[:, h, t, :], vs[:, h, t, :], start=False, stop=True)
                mm.then_inc(y_psum, 1)

            def y1_transpose(h):
                pe.wait_ge(y1_lo, h + 1)
                for t in range(NT):
                    mm = nc.tensor.transpose(p_yT[h][:, TT * t:TT * (t + 1)],
                                             y1s[:, h, t, :, :].rearrange("p a d -> p (a d)").bitcast(F32),
                                             ident[0:TT, 0:TT])
                mm.then_inc(yT_psum, 1)

            def logits(h):
                pe.wait_ge(yT_ready, h + 1)
                for t in range(NT):
                    mm = nc.tensor.matmul(p_lg[h][:, t, :].rearrange("p (a e) -> p a e", a=2),
                                          y1T[:, h, TT * t:TT * (t + 1)], wvg[:, :, D:D + E], start=True, stop=True)
                mm.then_inc(lg_psum, 1)

            def gates_transpose(h):
                pe.wait_ge(g_ready, h + 1)
                for t in range(NT):
                    mm = nc.tensor.transpose(p_gT[h][:, TT * t:TT * (t + 1)], g[:, h, t, :], ident[0:TT, 0:TT])
                mm.then_inc(gT_psum, 1)

            def expert_in(i):
                h, e = divmod(i, E)
                if i >= 4:
                    pe.wait_ge(hid_ready, i - 3)
                nc.tensor.matmul(p_hid[:, e % 4, :], w1_hi[:, e, :], y1T[:, h, :], start=True, stop=False)
                nc.tensor.matmul(p_hid[:, e % 4, :], w1_lo[:, e, :], y1T[:, h, :],
                                 start=False, stop=True).then_inc(hid_psum, 1)

            def expert_out(h, p):
                i = h * E + 2 * p
                pe.wait_ge(hid_ready, i + 2)
                for j in range(2):
                    mm = nc.tensor.matmul(p_moe[h][D * j:D * (j + 1), :], w2_sb[:, 2 * p + j, :],
                                          hid[:, (i + j) % NH, :], start=(p == 0), stop=(p == (PAIRS, SUMMED)[h] - 1))
                mm.then_inc(hid_used, 1)

            def combine_first(h):
                for t in range(NT):
                    cols = slice(TT * t, TT * (t + 1))
                    nc.tensor.matmul(p_fin[h][:, t, :], gT[:, h, cols], b2_sb[:, :], start=(t == 0), stop=False,
                                     skip_group_check=True)
                    nc.tensor.matmul(p_fin[h][:, t, :], y1T[:, h, cols], ident2_r[:, :], start=False, stop=False,
                                     skip_group_check=True)

            def combine(h):
                pe.wait_ge(moe_ready, h + 1)
                for t in range(NT):
                    cols = slice(TT * t, TT * (t + 1))
                    mm = nc.tensor.matmul(p_fin[h][:, t, :], moe[:, h, cols], ident2[:, :], start=False, stop=True,
                                          skip_group_check=True)
                mm.then_inc(fin_psum, 1)

            def expert_direct(e):
                i = E + e
                pe.wait_ge(hid_ready, i + 1)
                for t in range(NT):
                    nc.tensor.matmul(p_fin[1][:, t, :], hid[:, i % NH, TT * t:TT * (t + 1)],
                                     w2_sb[:, e, :], start=False, stop=False, skip_group_check=True)

            def keep_warm(n):
                for _ in range(n):
                    nc.tensor.matmul(banks[:, 4, :], zeros[:, 0:P], zeros[:, :], start=True, stop=True)

            pe.wait_ge(zeros_ready, 1)
            keep_warm(WARM)
            pe.wait_ge(qk_in, 16)
            nc.tensor.matmul(p_a, qk_sb[:, 0:2 * D], qk_sb[:, 2 * D:3 * D], start=True, stop=True).then_inc(a_psum, 1)
            pe.wait_ge(tokw_doubled, 1)
            embed(0, 0)
            embed(0, 1)
            embed(0, 2)
            embed(0, 3)
            embed(1, 0)
            pe.wait_ge(a_hi_ready, 1)
            pe.wait_ge(a_lo_ready, 1)
            project(0)
            scores(0)
            pe.wait_ge(wvg_lo_ready, 1)
            value_rows(0)
            embed(1, 1)
            embed(1, 2)
            embed(1, 3)
            pe.wait_ge(ident2_r_ready, 1)
            attend(0)
            project(1)
            scores(1)
            value_rows(1)
            pe.wait_ge(consts, 5)
            keep_warm(WARM_NORM)
            y1_transpose(0)
            keep_warm(WARM_COPY)
            logits(0)
            pe.wait_ge(w1_lo_ready, 1)
            expert_in(0)
            expert_in(1)
            keep_warm(WARM_VALUES)
            attend(1)
            keep_warm(WARM_GATES)
            gates_transpose(0)
            pe.wait_ge(gT_ready, 1)
            expert_in(2)
            expert_in(3)
            pe.wait_ge(b2_in, 16)
            combine_first(0)
            keep_warm(WARM_NORM_1)
            pe.wait_ge(w1_lo_ready, 2)
            pe.wait_ge(w2_in, 16)
            y1_transpose(1)
            keep_warm(WARM_COPY)
            logits(1)
            for p in range(PAIRS):
                expert_in(2 * p + 4)
                expert_in(2 * p + 5)
                expert_out(0, p)
                if p == 2:
                    gates_transpose(1)
            pe.wait_ge(gT_ready, 2)
            for p in range(SUMMED):
                if p + 2 < PAIRS:
                    expert_in(E + 2 * p + 4)
                    expert_in(E + 2 * p + 5)
                if p == 0:
                    combine(0)
                expert_out(1, p)
                if p == 1:
                    combine_first(1)
            for e in range(2 * SUMMED + 4, E):
                expert_in(E + e)
            for e in range(2 * SUMMED, E):
                expert_direct(e)
            combine(1)


def kernel(**inputs):
    import numpy as np
    import concourse.bacc as bacc
    from concourse.bass_utils import run_bass_kernel_spmd

    a = {k: np.asarray(v) for k, v in inputs.items()}
    x = a["x"]
    B, C, H, W = x.shape
    nh, nw = H // PATCH, W // PATCH
    D, K = a["L0_tok_W"].shape
    E, _, F = a["L0_ffn_w1"].shape
    tokens = B * nh * nw
    ch = K // 128
    xt = x.reshape(B, C, nh, PATCH, nw, PATCH).transpose(1, 3, 5, 0, 2, 4).reshape(ch, 128, 2, tokens // 2)
    arrays = {
        "x_kt": xt.transpose(1, 2, 0, 3),
        "tokw": a["L0_tok_W"].T.reshape(ch, 128, D).transpose(1, 0, 2),
        "qk": np.concatenate([a["L0_attn_Wq"], a["L0_attn_Wq"], a["L0_attn_Wk"]], axis=1),
        "wvgb": np.concatenate([a["L0_attn_Wv"].T, a["L0_ffn_gate_w"], a["L0_tok_b"][:, None]], axis=1),
        "w1": a["L0_ffn_w1"].transpose(1, 0, 2),
        "w2b1": np.concatenate([a["L0_ffn_w2"].transpose(1, 0, 2).reshape(F, E * D), a["L0_ffn_b1"].T], axis=1),
        "b2": a["L0_ffn_b2"],
        "rows": np.concatenate([a["L0_ffn_gate_b"], a["L0_ffn_gamma"], a["L0_ffn_beta"]]),
    }
    arrays = {k: np.ascontiguousarray(v) for k, v in arrays.items()}
    nc = bacc.Bacc("TRN2", target_bir_lowering=False, num_devices=1)
    args = [nc.dram_tensor(k, v.shape, mybir.dt.from_np(v.dtype), kind="ExternalInput").ap()
            for k, v in arrays.items()]
    out = nc.dram_tensor("out", (B, nh * nw, D), F32, kind="ExternalOutput").ap()
    vit_tower(nc, *args, out)
    r = run_bass_kernel_spmd(nc, [arrays], core_ids=[0])
    return r.results[0]["out"]
```
